# Optimizing a Trainium2 kernel written in Bass

```python
import numpy as np
import jax
import jax.numpy as jnp

def _softmax(x, axis=-1):
    return jax.nn.softmax(x, axis=axis)

def _gelu(x):
    return jax.nn.gelu(x, approximate=True)

def _silu(x):
    return jax.nn.silu(x)

def _sigmoid(x):
    return jax.nn.sigmoid(x)

def _layernorm(x, axis=-1, eps=1e-05):
    m = jnp.mean(x, axis=axis, keepdims=True)
    v = jnp.var(x, axis=axis, keepdims=True)
    return (x - m) / jnp.sqrt(v + eps)

def _scatter_add(tgt, idx, src, axis=0):
    return tgt.at[idx].add(src)

def _segment_sum(src, seg, n):
    return jax.ops.segment_sum(src, seg, n)
kernel_name = 'mk_conv_preact_d2_conv_nchw384_r4_29048f'

def setup_inputs(seed: int=0):
    np.random.seed(seed)
    _w = jnp.asarray

    def _rec_inputs():
        import jax
        import jax.numpy as jnp
        _gk = jax.random.key(seed)
        x = -0.0002221 + 1 * jax.random.normal(jax.random.fold_in(_gk, 1), (4, 96, 32, 32), jnp.float32)
        return x
    x = _rec_inputs()

    def _L0_conv_setup():
        import jax, jax.numpy as jnp
        import numpy as np
        NUM_HEADS = 8
        EPS = 1e-12

        def _l2norm(t):
            n = jnp.sqrt(jnp.sum(t * t, axis=-1, keepdims=True))
            return t / jnp.maximum(n, EPS)
        key = jax.random.key(seed)
        ks = jax.random.split(key, 4)
        c = 96
        x = jax.random.normal(ks[0], (4, c, 32, 32), dtype=jnp.float32)
        qkv_w = jax.random.normal(ks[1], (3 * c, c), dtype=jnp.float32) * (1.0 / np.sqrt(c))
        proj_w = jax.random.normal(ks[2], (c, c), dtype=jnp.float32) * (1.0 / np.sqrt(c))
        proj_b = jax.random.normal(ks[3], (c,), dtype=jnp.float32) * 0.01
        temperature = jnp.ones((NUM_HEADS, 1, 1), dtype=jnp.float32)
        return {'x': x, 'qkv_w': qkv_w, 'proj_w': proj_w, 'proj_b': proj_b, 'temperature': temperature}
    _L0_conv_all = _L0_conv_setup()
    _L0_conv_in = {k: v for k, v in _L0_conv_all.items() if k in ('qkv_w', 'proj_w', 'proj_b', 'temperature')}
    del _L0_conv_all

    def _L1_conv_setup():
        import jax, jax.numpy as jnp
        import numpy as np
        B, DIM, H, W = (2, 96, 64, 64)
        HID = DIM * 1
        P = 8
        key = jax.random.key(seed)
        k0, k1, k2, k3, k4 = jax.random.split(key, 5)
        x = jax.random.normal(k0, (B, DIM, H, W), jnp.float32)
        fft_filter = jax.random.normal(k1, (HID, P, P // 2 + 1), jnp.float32)
        w_in = jax.random.normal(k2, (HID, DIM), jnp.float32) * (1.0 / np.sqrt(DIM))
        w_dw = jax.random.normal(k3, (HID, 1, 3, 3), jnp.float32) * (1.0 / 3.0)
        w_out = jax.random.normal(k4, (DIM, HID // 2), jnp.float32) * (1.0 / np.sqrt(HID // 2))
        return {'x': x, 'fft_filter': fft_filter, 'w_in': w_in, 'w_dw': w_dw, 'w_out': w_out}
    _L1_conv_all = _L1_conv_setup()
    _L1_conv_in = {k: v for k, v in _L1_conv_all.items() if k in ('fft_filter', 'w_in', 'w_dw', 'w_out')}
    del _L1_conv_all
    return {'x': x, 'L0_conv_qkv_w': _L0_conv_in['qkv_w'], 'L0_conv_proj_w': _L0_conv_in['proj_w'], 'L0_conv_proj_b': _L0_conv_in['proj_b'], 'L0_conv_temperature': _L0_conv_in['temperature'], 'L1_conv_fft_filter': _L1_conv_in['fft_filter'], 'L1_conv_w_in': _L1_conv_in['w_in'], 'L1_conv_w_dw': _L1_conv_in['w_dw'], 'L1_conv_w_out': _L1_conv_in['w_out']}

def reference(x, L0_conv_qkv_w, L0_conv_proj_w, L0_conv_proj_b, L0_conv_temperature, L1_conv_fft_filter, L1_conv_w_in, L1_conv_w_dw, L1_conv_w_out):
    import jax
    import jax.numpy as jnp

    def _L0_conv_ref(x, qkv_w, proj_w, proj_b, temperature):
        import jax, jax.numpy as jnp
        import numpy as np
        NUM_HEADS = 8
        EPS = 1e-12

        def _l2norm(t):
            n = jnp.sqrt(jnp.sum(t * t, axis=-1, keepdims=True))
            return t / jnp.maximum(n, EPS)
        b, c, h, w = x.shape
        nh = NUM_HEADS
        hd = c // nh
        hw = h * w
        qkv = jnp.einsum('bchw,oc->bohw', x, qkv_w)
        q, k, v = jnp.split(qkv, 3, axis=1)
        q = q.reshape(b, nh, hd, hw)
        k = k.reshape(b, nh, hd, hw)
        v = v.reshape(b, nh, hd, hw)
        q = _l2norm(q)
        k = _l2norm(k)
        attn = jnp.einsum('bndt,bnet->bnde', q, k) * temperature
        attn = jax.nn.softmax(attn, axis=-1)
        out = jnp.einsum('bnde,bnet->bndt', attn, v).reshape(b, c, h, w)
        out = jnp.einsum('bchw,oc->bohw', out, proj_w) + proj_b[None, :, None, None]
        return out

    def _L1_conv_ref(x, fft_filter, w_in, w_dw, w_out):
        import jax, jax.numpy as jnp
        import numpy as np
        B, DIM, H, W = (2, 96, 64, 64)
        HID = DIM * 1
        P = 8
        b, c, h, w = x.shape
        hid = w_in.shape[0]
        hb, wb = (h // P, w // P)
        t = jnp.einsum('bchw,oc->bohw', x, w_in)
        tp = t.reshape(b, hid, hb, P, wb, P)
        tf = jnp.fft.rfft2(tp, axes=(3, 5))
        tf = tf * fft_filter[None, :, None, :, None, :]
        tp = jnp.fft.irfft2(tf, s=(P, P), axes=(3, 5))
        t = tp.reshape(b, hid, h, w)
        t = jax.lax.conv_general_dilated(t, w_dw, window_strides=(1, 1), padding='SAME', feature_group_count=hid, dimension_numbers=('NCHW', 'OIHW', 'NCHW'))
        x1, x2 = (t[:, :hid // 2], t[:, hid // 2:])
        g = jax.nn.gelu(x1, approximate=False) * x2
        return jnp.einsum('bchw,oc->bohw', g, w_out)

    def _gn(v, G=32, eps=1e-05):
        B_, C_, H_, W_ = v.shape
        g = v.reshape(B_, G, C_ // G, H_, W_)
        m = jnp.mean(g, axis=(2, 3, 4), keepdims=True)
        s = jnp.var(g, axis=(2, 3, 4), keepdims=True)
        return ((g - m) / jnp.sqrt(s + eps)).reshape(v.shape)

    def _ln_c(v, eps=1e-06):
        m = jnp.mean(v, axis=1, keepdims=True)
        s = jnp.var(v, axis=1, keepdims=True)
        return (v - m) / jnp.sqrt(s + eps)

    def _ln_t(v, eps=1e-05):
        m = jnp.mean(v, axis=-1, keepdims=True)
        s = jnp.var(v, axis=-1, keepdims=True)
        return (v - m) / jnp.sqrt(s + eps)

    def _to_tokens(v):
        B_, C_, H_, W_ = v.shape
        return v.reshape(B_, C_, H_ * W_).transpose(0, 2, 1)

    def _from_tokens(t, like):
        B_, C_, H_, W_ = like.shape
        return t.transpose(0, 2, 1).reshape(B_, C_, H_, W_)
    x = x + _L0_conv_ref(_gn(x), L0_conv_qkv_w, L0_conv_proj_w, L0_conv_proj_b, L0_conv_temperature)
    x = x + _L1_conv_ref(_gn(x), L1_conv_fft_filter, L1_conv_w_in, L1_conv_w_dw, L1_conv_w_out)
    return x

_drawn_inputs = setup_inputs


def setup_inputs(seed=0):
    import zlib

    import numpy as np

    out = dict(_drawn_inputs(seed))
    spreads = {'L0_conv_temperature': (1.0, 0.6)}
    factors = {'L0_conv_proj_b': 6.22}
    for name, (base, spread) in spreads.items():
        noise = np.random.default_rng([zlib.crc32(name.encode()), seed]).standard_normal(out[name].shape)
        drawn = base * np.exp(spread * noise) if base else spread * noise
        out[name] = jnp.asarray(drawn.astype(out[name].dtype))
    for name, factor in factors.items():
        out[name] = (out[name] * factor).astype(out[name].dtype)
    return out
```

```python
import math
from contextlib import ExitStack

import numpy as np

import concourse.bass as bass
from concourse import mybir

ALU = mybir.AluOpType
ACT = mybir.ActivationFunctionType
AX = mybir.AxisListType
F32 = mybir.dt.float32

B, C, H, W = 4, 96, 32, 32
PIX = H * W
HEADS = 8
HD = C // HEADS
GROUP = C // 32
EPS = 1e-5
L2_EPS = 1e-12
P = 8
FREQ = P * P
HALF = PIX // 2
STRIP = 128
STRIPS = HALF // STRIP
GATED = C // 2
GELU_AT = 64
LANES = GELU_AT + GATED
TAPS = 9
PE_TAPS = (1, 1, 1, 1)
PW = W + 2
ROWS = H // 2
MASKED = -1e30


def frequencies():
    own = [(0, 0), (0, 4), (4, 0), (4, 4)]
    pairs = [(ky, kx) for kx in (1, 2, 3) for ky in range(P)] + [(ky, kx) for kx in (0, 4) for ky in (1, 2, 3)]
    return own, pairs


def basis():
    own, pairs = frequencies()
    y, x = np.meshgrid(np.arange(P), np.arange(P), indexing="ij")
    waves, back = [], []
    for ky, kx in own:
        waves.append(np.cos(2 * math.pi * (ky * y + kx * x) / P))
        back.append(1 / FREQ)
    for ky, kx in pairs:
        for wave in (np.cos, np.sin):
            waves.append(wave(2 * math.pi * (ky * y + kx * x) / P))
            back.append(2 / FREQ)
    return np.stack([w.ravel() for w in waves], 1), np.array(back)


def both_patches(block):
    out = np.zeros((2 * FREQ, 2 * FREQ), np.float32)
    out[:FREQ, :FREQ] = block
    out[FREQ:, FREQ:] = block
    return out


def filter_selection():
    own, pairs = frequencies()
    keys = own + [k for k in pairs for _ in range(2)]
    out = np.zeros((P * (P // 2 + 1), 2 * FREQ), np.float32)
    for f, (ky, kx) in enumerate(keys):
        for row in {ky, (-ky) % P} if kx in (0, 4) else {ky}:
            share = 0.5 if kx in (0, 4) and ky not in (0, 4) else 1.0
            out[row * (P // 2 + 1) + kx, f] = out[row * (P // 2 + 1) + kx, FREQ + f] = share
    return out


K_IDENT, K_GROUP, K_MASK, K_DFT, K_BACK, K_SEL = 0, 112, 208, 304, 432, 560
K_EARLY = 208
K_ALL = 688


def constants():
    waves, back = basis()
    out = np.zeros((128, K_ALL), np.float32)
    out[:LANES, K_IDENT:K_IDENT + LANES] = np.eye(LANES)
    out[:C, K_GROUP:K_GROUP + C] = np.kron(np.eye(C // GROUP), np.full((GROUP, GROUP), 1 / GROUP))
    out[:C, K_MASK:K_MASK + C] = MASKED * (1 - np.kron(np.eye(HEADS), np.ones((HD, HD))))
    out[:, K_DFT:K_DFT + 128] = both_patches(waves)
    out[:, K_BACK:K_BACK + 128] = both_patches((waves * back).T)
    out[:P * (P // 2 + 1), K_SEL:K_SEL + 128] = filter_selection()
    return out


def unit_spectrum():
    out = np.zeros((1, B * PIX), np.float32)
    out[0, ::FREQ] = FREQ
    return out


def weave(chain, fill):
    out, done = [], 0
    for n, step in enumerate(chain):
        out.append(step)
        upto = (n + 1) * len(fill) // len(chain)
        out += fill[done:upto]
        done = upto
    return out


CHAIN = ("project", "logits", "softmax", "attend", "mix", "second", "square", "group", "fold")


def make_order():
    def head(b):
        return [("turn", b, 0), ("turn", b, 1), ("gram", b)]

    def chains(*images):
        return [(s, b) for s in CHAIN for b in images]

    def spectrum(b):
        return [("spec", b, 0), ("spec", b, 1)]

    def front(b):
        return [("filter", b, 0), ("filter", b, 1), ("back", b, 0), ("back", b, 1), ("conv", b)]

    def taps(b):
        return [("tap", b, t) for t in range(PE_TAPS[b], TAPS)]

    def rear(b):
        return [("gate", b), ("final", b, 0), ("final", b, 1)]

    order = [("stats", 0), ("var", 0), ("norm", 0), ("stats", 1), ("var", 1), ("norm", 1)] + head(0)
    order += [("stats", 2), ("var", 2), ("norm", 2)] + head(1) + [("setup", 0), ("stats", 3), ("var", 3), ("norm", 3)]
    order += weave(chains(0, 1), spectrum(0) + head(2) + spectrum(1) + head(3) + spectrum(2))
    order += weave(chains(2, 3), front(0) + taps(0)[:4] + front(1) + spectrum(3) + taps(0)[4:])
    order += weave(taps(1), rear(0) + front(2))
    order += weave(taps(2), rear(1) + front(3))
    order += weave(taps(3), rear(2)) + rear(3)
    return order


ORDER = make_order()
A_STEPS = [s for s in ORDER if s[0] in ("turn", "spec", "back", "final")]
V_STEPS = [s for s in ORDER if s[0] == "filter"]
T_STEPS = [s for s in ORDER if s[0] == "tap"]


def through(steps, step):
    return steps.index(step) + 1


def build(nc, x, wqkT, wv, projT, proj_b, temp, filt, w_inT, w_outT, w_dw, consts, unit, out):
    with ExitStack() as ctx:
        def sb(name, shape):
            return ctx.enter_context(nc.sbuf_tensor(name, shape, F32))

        def sem(name):
            return ctx.enter_context(nc.semaphore(name))

        X = sb("X", [C, B, PIX])
        XN = sb("XN", [C, B, PIX])
        XNT = sb("XNT", [STRIP, B, 2 * STRIPS, C])
        XF = sb("XF", [C + 1, B, PIX])
        Z = sb("Z", [STRIP, B, 2 * STRIPS, LANES])
        PAD = sb("PAD", [LANES, B, H + 2, PW])
        ACC = sb("ACC", [LANES, B, PIX])
        GE = sb("GE", [GATED, B, PIX])
        GT = sb("GT", [GATED, B, PIX])

        CST = sb("CST", [128, K_ALL])
        WQK = sb("WQK", [C, 2 * C])
        WV = sb("WV", [C, C])
        PRJ = sb("PRJ", [C, C])
        WIN = sb("WIN", [C, C])
        WOUT = sb("WOUT", [GATED, C])
        FLT = sb("FLT", [P * (P // 2 + 1), C])
        FREAL = sb("FREAL", [2 * FREQ, C])
        DW = sb("DW", [LANES, TAPS])
        DIAG = sb("DIAG", [LANES, max(PE_TAPS), LANES])
        PB = sb("PB", [C, 1])
        TEMP = sb("TEMP", [C, 1])
        ONES = sb("ONES", [C, 1])
        MEANW = sb("MEANW", [C, 1])
        POWER = sb("POWER", [C, 2])
        WARM = sb("WARM", [1, 2])

        BN = sb("BN", [C, B, 2, 6])
        MV = sb("MV", [C, B, 2])
        SG = sb("SG", [C, B, 2])
        ST = sb("ST", [C, B, 16])
        NEGVAR, VAR, RSTD, STD, SHIFT, MEANXN, BIAS, RQ, NMAX, SUM, RSUM, TT, NV2, V2E, R2 = (
            range(15))
        G = sb("G", [C, B, C])
        TK = sb("TK", [C, B, C])
        QQ = sb("QQ", [C, B, 2 * C])
        NRM = sb("NRM", [C, B, 2])
        RN = sb("RN", [C, B, 2])
        KL = sb("KL", [C, B, C])
        LM = sb("LM", [C, B, C])
        PR = sb("PR", [C, B, C])
        PJ = sb("PJ", [C, B, C])
        Q1 = sb("Q1", [C, B, C])
        A = sb("A", [C, B, C + 1])
        AT = sb("AT", [C, B, C])
        AGA = sb("AGA", [C, B, C])
        S2 = sb("S2", [C, B, 2])
        SG2 = sb("SG2", [C, B, 2])
        WI = sb("WI", [C, B, C])
        BT = sb("BT", [C + 1, B, C])

        def col(b, which):
            return ST[:, b, which:which + 1]

        CH = [ctx.enter_context(nc.psum_tensor(f"CH{i}", [128, 512], F32)) for i in range(2)]
        AB = [ctx.enter_context(nc.psum_tensor(f"AB{i}", [128, 512], F32)) for i in range(2)]
        VB = [ctx.enter_context(nc.psum_tensor(f"VB{i}", [128, 512], F32)) for i in range(2)]
        CV = ctx.enter_context(nc.psum_tensor("CV", [128, 2, 512], F32))

        x_in = [sem(f"x_in{b}") for b in range(B)]
        early_in, weights_in, late_in = sem("early_in"), sem("weights_in"), sem("late_in")
        pool_set = sem("pool_set")
        diag_set, filter_sum, filter_set = sem("diag_set"), sem("filter_sum"), sem("filter_set")
        v_done = sem("v_done")
        stats_set, group_mean = sem("stats_set"), sem("group_mean")
        shift_set, std_set, bias_set = sem("shift_set"), sem("std_set"), sem("bias_set")
        var_set, rstd_set, xn_set, mean_set = sem("var_set"), sem("rstd_set"), sem("xn_set"), sem("mean_set")
        gram_sum, gram_set = sem("gram_sum"), sem("gram_set")
        qk_sum, qk_set, logit_sum = sem("qk_sum"), sem("qk_set"), sem("logit_sum")
        norm_set, rnorm_set, logit_set = sem("norm_set"), sem("rnorm_set"), sem("logit_set")
        kl_set, turned_sum = sem("kl_set"), sem("turned_sum")
        rq_set = sem("rq_set")
        exp_set, attn_set = sem("exp_set"), sem("attn_set")
        q1_sum, q1_set, m_sum, a_set = sem("q1_sum"), sem("q1_set"), sem("m_sum"), sem("a_set")
        ag_sum, aga_set, square_sum, s2_set = sem("ag_sum"), sem("aga_set"), sem("square_sum"), sem("s2_set")
        group2_sum, var2_set, rstd2_set, wi_set = sem("group2_sum"), sem("var2_set"), sem("rstd2_set"), sem("wi_set")
        bt_sum, bt_set = sem("bt_sum"), sem("bt_set")
        a_full, a_free = sem("a_full"), sem("a_free")
        v_full, v_free = sem("v_full"), sem("v_free")
        conv_sum, tap_set = sem("conv_sum"), sem("tap_set")
        gelu_set, gate_set = sem("gelu_set"), sem("gate_set")
        stored = sem("stored")

        block = ctx.enter_context(nc.Block())

        @block.sync
        def _(sp):
            sp.dma_start(X[:, 0, :], x[0]).then_inc(x_in[0], 16)
            sp.dma_start(CST[:, 0:K_EARLY], consts[:, 0:K_EARLY]).then_inc(early_in, 16)
            for b in range(1, B):
                sp.dma_start(X[:, b, :], x[b]).then_inc(x_in[b], 16)
            for step in ORDER:
                if step[0] == "final":
                    _, b, h = step
                    sp.wait_ge(a_free, through(A_STEPS, step))
                    sp.dma_start(out[b][:, HALF * h:HALF * (h + 1)],
                                 X[:, b, HALF * h:HALF * (h + 1)]).then_inc(stored, 16)
            sp.wait_ge(stored, 16 * 2 * B)

        @block.gpsimd
        def _(pool):
            nc.gpsimd.memset(POWER[:], -0.5).then_inc(pool_set, 1)
            nc.gpsimd.memset(ONES[:], 1.0).then_inc(pool_set, 1)
            nc.gpsimd.memset(MEANW[:], 1.0 / PIX).then_inc(pool_set, 1)
            nc.gpsimd.memset(Z[:, :, :, GATED:GELU_AT].rearrange("p b s z -> p (b s) z"),
                             0.0).then_inc(pool_set, 1)
            nc.gpsimd.memset(PAD[:, :, 0::H + 1, :], 0.0).then_inc(pool_set, 1)
            nc.gpsimd.memset(PAD[:, :, 1:H + 1, 0::PW - 1], 0.0).then_inc(pool_set, 1)
            pool.wait_ge(pool_set, 2)
            nc.gpsimd.tensor_tensor(WARM[:, 1:2], ONES[0:1, 0:1], POWER[0:1, 0:1], ALU.pow)
            for step in ORDER:
                b = step[1]
                if step[0] == "var":
                    pool.wait_ge(var_set, b + 1)
                    nc.gpsimd.tensor_tensor(col(b, RSTD), col(b, VAR), POWER[:, 0:1], ALU.pow).then_inc(rstd_set, 1)
                elif step[0] == "logits":
                    pool.wait_ge(norm_set, b + 1)
                    nc.gpsimd.tensor_tensor(RN[:, b, :], NRM[:, b, :], POWER[:], ALU.pow).then_inc(rnorm_set, 1)
                elif step[0] == "group":
                    pool.wait_ge(var2_set, b + 1)
                    nc.gpsimd.tensor_tensor(col(b, R2), col(b, V2E), POWER[:, 0:1], ALU.pow).then_inc(rstd2_set, 1)

        @block.scalar
        def _(act):
            act.dma_start(WQK[:], wqkT).then_inc(weights_in, 16)
            act.dma_start(WV[:], wv).then_inc(weights_in, 16)
            act.dma_start(PRJ[:], projT).then_inc(weights_in, 16)
            act.dma_start(PB[:], proj_b).then_inc(weights_in, 16)
            act.dma_start(TEMP[:], temp).then_inc(weights_in, 16)
            act.dma_start(WIN[:], w_inT).then_inc(weights_in, 16)
            act.dma_start(CST[:, K_EARLY:K_ALL], consts[:, K_EARLY:K_ALL]).then_inc(late_in, 16)
            act.dma_start(FLT[:], filt).then_inc(late_in, 16)
            act.dma_start(DW[:], w_dw).then_inc(late_in, 16)
            act.dma_start(WOUT[:], w_outT).then_inc(late_in, 16)
            act.dma_start(XF[C:C + 1, :, :].rearrange("p b n -> p (b n)"), unit).then_inc(late_in, 16)
            act.wait_ge(pool_set, 1)
            nc.scalar.activation(WARM[:, 0:1], POWER[0:1, 0:1], ACT.Exp)
            n = 0
            for step in ORDER:
                b = step[1]
                if step[0] in ("turn", "spec", "back", "final"):
                    h = step[2]
                    bank = AB[n % 2]
                    n += 1
                    act.wait_ge(a_full, n)
                    bias, func = 0.0, ACT.Copy
                    if step[0] == "turn":
                        dst = XNT[:, b, STRIPS * h:STRIPS * (h + 1), :]
                        src = bank[:, 0:STRIPS * C].rearrange("p (s c) -> p s c", c=C)
                    elif step[0] == "spec":
                        dst, src = XF[0:C, b, HALF * h:HALF * (h + 1)], bank[0:C, :]
                    elif step[0] == "back":
                        if b == 0 and h == 0:
                            act.wait_ge(pool_set, 6)
                        dst = PAD[:, b, 1 + ROWS * h:1 + ROWS * (h + 1), 1:1 + W]
                        src = bank[0:LANES, :].rearrange("c (y x) -> c y x", x=W)
                    else:
                        dst, src = X[:, b, HALF * h:HALF * (h + 1)], bank[0:C, :]
                        bias, func = col(b, BIAS), ACT.Identity
                    nc.scalar.activation(dst, src, func, bias=bias).then_inc(a_free, 1)
                elif step[0] == "norm":
                    act.wait_ge(shift_set, b + 1)
                    nc.scalar.activation(XN[:, b, :], X[:, b, :], ACT.Identity, bias=col(b, SHIFT),
                                         scale=col(b, RSTD)).then_inc(xn_set, 1)
                elif step[0] == "softmax":
                    act.wait_ge(logit_set, b + 1)
                    nc.scalar.activation(PR[:, b, :], LM[:, b, :], ACT.Exp, bias=col(b, NMAX),
                                         accum_out=col(b, SUM)).then_inc(exp_set, 1)
                elif step[0] == "gate":
                    act.wait_ge(tap_set, through(T_STEPS, ("tap", b, TAPS - 1)))
                    nc.scalar.activation(GE[:, b, :], ACC[GELU_AT:LANES, b, :], ACT.Gelu).then_inc(gelu_set, 1)

        @block.vector
        def _(dve):
            done = [0]

            def then(ins):
                done[0] += 1
                ins.then_inc(v_done, 1)
                dve.wait_ge(v_done, done[0])

            v = nc.vector
            for step in ORDER:
                name, b = step[0], step[1]
                ps = CH[b % 2]
                if name == "stats":
                    dve.wait_ge(x_in[b], 16)
                    for h in range(2):
                        ins = v.bn_stats(BN[:, b, h, :], X[:, b, HALF * h:HALF * (h + 1)])
                        then(ins)
                    then(v.bn_aggr(MV[:, b, :], BN[:, b, :, :].rearrange("p h s -> p (h s)")))
                    v.scalar_tensor_tensor(MV[:, b, 1:2], MV[:, b, 0:1], MV[:, b, 0:1], MV[:, b, 1:2],
                                           ALU.mult, ALU.add).then_inc(stats_set, 1)
                elif name == "var":
                    dve.wait_ge(group_mean, b + 1)
                    then(v.tensor_copy(SG[:, b, :], CV[0:C, 1, 2 * b:2 * b + 2]))
                    then(v.scalar_tensor_tensor(col(b, NEGVAR), SG[:, b, 0:1], SG[:, b, 0:1], SG[:, b, 1:2],
                                                ALU.mult, ALU.subtract))
                    v.tensor_scalar(col(b, VAR), col(b, NEGVAR), -1.0, EPS, ALU.mult, ALU.add).then_inc(var_set, 1)
                elif name == "norm":
                    dve.wait_ge(rstd_set, b + 1)
                    v.scalar_tensor_tensor(col(b, SHIFT), SG[:, b, 0:1], -1.0, col(b, RSTD),
                                           ALU.mult, ALU.mult).then_inc(shift_set, 1)
                    dve.wait_ge(shift_set, b + 1)
                    v.tensor_scalar(col(b, MEANXN), MV[:, b, 0:1], col(b, RSTD), col(b, SHIFT),
                                    ALU.mult, ALU.add).then_inc(mean_set, 1)
                    v.tensor_tensor(col(b, STD), col(b, VAR), col(b, RSTD), ALU.mult).then_inc(std_set, 1)
                elif name == "setup":
                    dve.wait_ge(filter_sum, 1)
                    v.tensor_copy(FREAL[:], VB[0][:, 0:C]).then_inc(filter_set, 1)
                    dve.wait_ge(late_in, 16 * 5)
                    for t in range(max(PE_TAPS)):
                        v.tensor_scalar(DIAG[:, t, :], CST[0:LANES, K_IDENT:K_IDENT + LANES], DW[:, t:t + 1],
                                        None, ALU.mult).then_inc(diag_set, 1)
                elif name == "gram":
                    dve.wait_ge(gram_sum, b + 1)
                    v.tensor_copy(G[:, b, :], CV[0:C, 0, 0:C]).then_inc(gram_set, 1)
                    if b == 0:
                        dve.wait_ge(weights_in, 16 * 6)
                    v.tensor_tensor(col(b, BIAS), SG[:, b, 0:1], PB[:], ALU.add).then_inc(bias_set, 1)
                elif name == "project":
                    dve.wait_ge(qk_sum, b + 1)
                    v.tensor_copy(TK[:, b, :], ps[0:C, C:2 * C]).then_inc(qk_set, 1)
                    v.tensor_tensor(QQ[:, b, :], WQK[:], ps[0:C, 0:2 * C], ALU.mult).then_inc(qk_set, 1)
                elif name == "logits":
                    dve.wait_ge(logit_sum, b + 1)
                    v.tensor_scalar(NRM[:, b, :], ps[0:C, 384:386], L2_EPS * L2_EPS, None,
                                    ALU.max).then_inc(norm_set, 1)
                    dve.wait_ge(rnorm_set, b + 1)
                    v.tensor_scalar(KL[:, b, :], ps[0:C, 192:192 + C], RN[:, b, 1:2], None,
                                    ALU.mult).then_inc(kl_set, 1)
                    v.tensor_tensor(col(b, RQ), RN[:, b, 0:1], TEMP[:], ALU.mult).then_inc(rq_set, 1)
                elif name == "softmax":
                    dve.wait_ge(turned_sum, b + 1)
                    dve.wait_ge(rq_set, b + 1)
                    then(v.scalar_tensor_tensor(LM[:, b, :], ps[0:C, 288:288 + C], col(b, RQ),
                                                CST[0:C, K_MASK:K_MASK + C], ALU.mult, ALU.add))
                    v.tensor_reduce(col(b, NMAX), LM[:, b, :], AX.X, ALU.max, negate=True).then_inc(logit_set, 1)
                elif name == "attend":
                    dve.wait_ge(exp_set, b + 1)
                    then(v.reciprocal(col(b, RSUM), col(b, SUM)))
                    v.tensor_scalar(PJ[:, b, :], PRJ[:], col(b, RSUM), None, ALU.mult).then_inc(attn_set, 1)
                    dve.wait_ge(q1_sum, b + 1)
                    v.tensor_copy(Q1[:, b, :], ps[0:C, 0:C]).then_inc(q1_set, 1)
                elif name == "mix":
                    dve.wait_ge(m_sum, b + 1)
                    dve.wait_ge(std_set, b + 1)
                    v.scalar_tensor_tensor(AT[:, b, :], CST[0:C, K_IDENT:K_IDENT + C], col(b, STD),
                                           ps[0:C, 192:192 + C], ALU.mult, ALU.add).then_inc(a_set, 1)
                    v.scalar_tensor_tensor(A[:, b, 0:C], CST[0:C, K_IDENT:K_IDENT + C], col(b, STD),
                                           ps[0:C, 96:96 + C], ALU.mult, ALU.add).then_inc(a_set, 1)
                elif name == "second":
                    dve.wait_ge(ag_sum, b + 1)
                    v.tensor_tensor(AGA[:, b, :], AT[:, b, :], ps[0:C, 288:288 + C], ALU.mult).then_inc(aga_set, 1)
                elif name == "square":
                    dve.wait_ge(square_sum, b + 1)
                    then(v.tensor_scalar(S2[:, b, 0:1], ps[0:C, 384:385], PB[:, 0:1], None, ALU.add))
                    then(v.tensor_tensor(col(b, TT), S2[:, b, 0:1], ps[0:C, 384:385], ALU.add))
                    v.scalar_tensor_tensor(S2[:, b, 1:2], col(b, TT), PB[:, 0:1], ps[0:C, 385:386],
                                           ALU.mult, ALU.add).then_inc(s2_set, 1)
                elif name == "group":
                    dve.wait_ge(group2_sum, b + 1)
                    then(v.tensor_copy(SG2[:, b, :], ps[0:C, 480:482]))
                    then(v.scalar_tensor_tensor(col(b, NV2), SG2[:, b, 0:1], SG2[:, b, 0:1], SG2[:, b, 1:2],
                                                ALU.mult, ALU.subtract))
                    v.tensor_scalar(col(b, V2E), col(b, NV2), -1.0, EPS, ALU.mult, ALU.add).then_inc(var2_set, 1)
                    v.tensor_scalar(A[:, b, C:C + 1], SG2[:, b, 0:1], -1.0, PB[:, 0:1],
                                    ALU.mult, ALU.add).then_inc(wi_set, 1)
                    dve.wait_ge(rstd2_set, b + 1)
                    v.tensor_scalar(WI[:, b, :], WIN[:], col(b, R2), None, ALU.mult).then_inc(wi_set, 1)
                elif name == "fold":
                    dve.wait_ge(bt_sum, b + 1)
                    v.tensor_copy(BT[:, b, :], ps[0:C + 1, 0:C]).then_inc(bt_set, 1)
                elif name == "filter":
                    h, n = step[2], through(V_STEPS, step)
                    dve.wait_ge(v_full, n)
                    if b == 0 and h == 0:
                        dve.wait_ge(filter_set, 1)
                    zs = Z[:, b, STRIPS * h:STRIPS * (h + 1), :]
                    for first, at in ((0, 0), (GATED, GELU_AT)):
                        ins = v.tensor_tensor(
                            zs[:, :, at:at + GATED],
                            VB[(n - 1) % 2][:, 0:STRIPS * C].rearrange("p (s c) -> p s c", c=C)[
                                :, :, first:first + GATED],
                            FREAL[:, first:first + GATED].unsqueeze(1).broadcast_to([2 * FREQ, STRIPS, GATED]),
                            ALU.mult)
                    ins.then_inc(v_free, 1)
                elif name == "tap":
                    t, n = step[2], through(T_STEPS, step)
                    first = t == PE_TAPS[b]
                    if first:
                        dve.wait_ge(conv_sum, b + 1)
                    else:
                        dve.wait_ge(tap_set, through(T_STEPS, ("tap", b, t - 1)))
                    acc = ACC[:, b, :].rearrange("c (y x) -> c y x", x=W)
                    before = CV[0:LANES, :, :].rearrange("c h (y x) -> c (h y) x", x=W) if first else acc
                    dy, dx = divmod(t, 3)
                    v.scalar_tensor_tensor(acc, PAD[:, b, dy:dy + H, dx:dx + W], DW[:, t:t + 1], before,
                                           ALU.mult, ALU.add).then_inc(tap_set, 1)
                elif name == "gate":
                    dve.wait_ge(gelu_set, b + 1)
                    v.tensor_tensor(GT[:, b, :], GE[:, b, :], ACC[0:GATED, b, :], ALU.mult).then_inc(gate_set, 1)

        @block.tensor
        def _(pe):
            def mm(o, lhsT, rhs, start=True, stop=True):
                return nc.tensor.matmul(o, lhsT, rhs, start=start, stop=stop)

            ident = CST[0:C, K_IDENT:K_IDENT + C]
            group = CST[0:C, K_GROUP:K_GROUP + C]
            for step in ORDER:
                name, b = step[0], step[1]
                ps = CH[b % 2]
                if name in ("turn", "spec", "back", "final"):
                    h, n = step[2], through(A_STEPS, step)
                    bank = AB[(n - 1) % 2]
                    if n > 2:
                        pe.wait_ge(a_free, n - 2)
                    if name == "turn":
                        pe.wait_ge(xn_set, b + 1)
                        for s in range(STRIPS):
                            at = HALF * h + STRIP * s
                            ins = nc.tensor.transpose(bank[:, C * s:C * (s + 1)], XN[:, b, at:at + STRIP], ident)
                    elif name == "spec":
                        pe.wait_ge(a_free, through(A_STEPS, ("turn", b, h)))
                        if b == 0 and h == 0:
                            pe.wait_ge(late_in, 16 * 5)
                        for s in range(STRIPS):
                            ins = mm(bank[0:C, STRIP * s:STRIP * (s + 1)], XNT[:, b, STRIPS * h + s, :],
                                     CST[:, K_DFT:K_DFT + 128])
                    elif name == "back":
                        pe.wait_ge(v_free, through(V_STEPS, ("filter", b, h)))
                        if b == 0 and h == 0:
                            pe.wait_ge(pool_set, 4)
                        rows = bank[0:LANES, :].rearrange("c (y s x) -> c s y x", s=STRIPS, x=P)
                        for s in range(STRIPS):
                            ins = mm(rows[:, s], Z[:, b, STRIPS * h + s, :], CST[:, K_BACK:K_BACK + 128])
                    else:
                        if b == 0 and h == 0:
                            pe.wait_ge(bias_set, B)
                        mm(bank[0:C, :], AT[:, b, :], XN[:, b, HALF * h:HALF * (h + 1)], stop=False)
                        pe.wait_ge(gate_set, b + 1)
                        ins = mm(bank[0:C, :], WOUT[:],
                                 GT[:, b, :].rearrange("p (h y s x) -> p h s y x", h=2, y=ROWS, x=P)[:, h],
                                 start=False)
                    ins.then_inc(a_full, 1)
                elif name == "stats":
                    pe.wait_ge(stats_set, b + 1)
                    if b == 0:
                        pe.wait_ge(early_in, 16)
                    mm(CV[0:C, 1, 2 * b:2 * b + 2], group, MV[:, b, :]).then_inc(group_mean, 1)
                elif name == "gram":
                    pe.wait_ge(a_free, through(A_STEPS, ("turn", b, 1)))
                    if b:
                        pe.wait_ge(gram_set, b)
                    for s in range(2 * STRIPS):
                        ins = mm(CV[0:C, 0, 0:C], XNT[:, b, s, :], XNT[:, b, s, :], start=(s == 0),
                                 stop=(s == 2 * STRIPS - 1))
                    ins.then_inc(gram_sum, 1)
                elif name == "setup":
                    pe.wait_ge(late_in, 16 * 5)
                    mm(VB[0][:, 0:C], CST[0:P * (P // 2 + 1), K_SEL:K_SEL + 128], FLT[:]).then_inc(filter_sum, 1)
                elif name == "project":
                    pe.wait_ge(gram_set, b + 1)
                    if b == 0:
                        pe.wait_ge(weights_in, 16 * 6)
                        pe.wait_ge(pool_set, 3)
                    if b >= 2:
                        pe.wait_ge(bt_set, b - 1)
                    mm(ps[0:C, 0:2 * C], G[:, b, :], WQK[:]).then_inc(qk_sum, 1)
                elif name == "logits":
                    pe.wait_ge(qk_set, 2 * (b + 1))
                    mm(ps[0:C, 384:385], QQ[:, b, 0:C], ONES[:])
                    mm(ps[0:C, 385:386], QQ[:, b, C:2 * C], ONES[:])
                    mm(ps[0:C, 192:192 + C], TK[:, b, :], WQK[:, 0:C]).then_inc(logit_sum, 1)
                elif name == "softmax":
                    pe.wait_ge(kl_set, b + 1)
                    mm(ps[0:C, 288:288 + C], KL[:, b, :], ident).then_inc(turned_sum, 1)
                elif name == "attend":
                    pe.wait_ge(attn_set, b + 1)
                    mm(ps[0:C, 0:C], PR[:, b, :], PJ[:, b, :]).then_inc(q1_sum, 1)
                elif name == "mix":
                    pe.wait_ge(q1_set, b + 1)
                    mm(ps[0:C, 192:192 + C], WV[:], Q1[:, b, :])
                    mm(ps[0:C, 96:96 + C], Q1[:, b, :], WV[:]).then_inc(m_sum, 1)
                elif name == "second":
                    pe.wait_ge(a_set, 2 * (b + 1))
                    pe.wait_ge(mean_set, b + 1)
                    mm(ps[0:C, 384:385], AT[:, b, :], col(b, MEANXN))
                    mm(ps[0:C, 288:288 + C], G[:, b, :], AT[:, b, :]).then_inc(ag_sum, 1)
                elif name == "square":
                    pe.wait_ge(aga_set, b + 1)
                    mm(ps[0:C, 385:386], AGA[:, b, :], MEANW[:]).then_inc(square_sum, 1)
                elif name == "group":
                    pe.wait_ge(s2_set, b + 1)
                    mm(ps[0:C, 480:482], group, S2[:, b, :]).then_inc(group2_sum, 1)
                elif name == "fold":
                    pe.wait_ge(wi_set, 2 * (b + 1))
                    mm(ps[0:C + 1, 0:C], A[:, b, :], WI[:, b, :]).then_inc(bt_sum, 1)
                elif name == "filter":
                    h, n = step[2], through(V_STEPS, step)
                    pe.wait_ge(bt_set, b + 1)
                    pe.wait_ge(a_free, through(A_STEPS, ("spec", b, h)))
                    pe.wait_ge(filter_set, 1)
                    if n > 2:
                        pe.wait_ge(v_free, n - 2)
                    for s in range(STRIPS):
                        at = HALF * h + STRIP * s
                        ins = mm(VB[(n - 1) % 2][:, C * s:C * (s + 1)], XF[:, b, at:at + STRIP], BT[:, b, :])
                    ins.then_inc(v_full, 1)
                elif name == "conv":
                    pe.wait_ge(a_free, through(A_STEPS, ("back", b, 1)))
                    if b == 0:
                        pe.wait_ge(gram_set, B)
                        pe.wait_ge(var_set, B)
                        pe.wait_ge(diag_set, max(PE_TAPS))
                    else:
                        pe.wait_ge(tap_set, through(T_STEPS, ("tap", b - 1, PE_TAPS[b - 1])))
                    for h in range(2):
                        for t in range(PE_TAPS[b]):
                            dy, dx = divmod(t, 3)
                            ins = mm(CV[0:LANES, h, :], DIAG[:, t, :],
                                     PAD[:, b, ROWS * h + dy:ROWS * (h + 1) + dy, dx:dx + W],
                                     start=(t == 0), stop=(t == PE_TAPS[b] - 1))
                    ins.then_inc(conv_sum, 1)



def kernel(**inputs):
    import concourse.bacc as bacc
    from concourse.bass_utils import run_bass_kernel_spmd

    f32 = np.float32
    qkv = np.asarray(inputs["L0_conv_qkv_w"])
    w_out = np.asarray(inputs["L1_conv_w_out"])
    gates_first = np.r_[GATED:C, 0:GATED]
    dw = np.zeros((LANES, TAPS), f32)
    dw[:GATED] = np.asarray(inputs["L1_conv_w_dw"]).reshape(C, TAPS)[GATED:]
    dw[GELU_AT:] = np.asarray(inputs["L1_conv_w_dw"]).reshape(C, TAPS)[:GATED]
    x = np.asarray(inputs["x"]).reshape(B, C, 2, ROWS, STRIPS, P).transpose(0, 1, 2, 4, 3, 5)
    arrays = {
        "x": x.reshape(B, C, PIX),
        "wqkT": qkv[:2 * C].T,
        "wv": qkv[2 * C:],
        "projT": np.asarray(inputs["L0_conv_proj_w"]).T,
        "proj_b": np.asarray(inputs["L0_conv_proj_b"]).reshape(C, 1),
        "temp": np.repeat(np.asarray(inputs["L0_conv_temperature"]).reshape(HEADS), HD).reshape(C, 1),
        "filt": np.asarray(inputs["L1_conv_fft_filter"]).reshape(C, P * (P // 2 + 1)).T[:, gates_first],
        "w_inT": np.asarray(inputs["L1_conv_w_in"]).T[:, gates_first],
        "w_outT": w_out.T,
        "w_dw": dw,
        "consts": constants(),
        "unit": unit_spectrum(),
    }
    arrays = {f"in_{k}": np.ascontiguousarray(v) for k, v in arrays.items()}
    nc = bacc.Bacc("TRN2", target_bir_lowering=False, num_devices=1)
    args = [nc.dram_tensor(k, v.shape, mybir.dt.from_np(v.dtype), kind="ExternalInput").ap()
            for k, v in arrays.items()]
    out = nc.dram_tensor("out", [B, C, PIX], F32, kind="ExternalOutput").ap()
    build(nc, *args, out)
    r = run_bass_kernel_spmd(nc, [arrays], core_ids=[0])
    got = np.asarray(r.results[0]["out"])
    return got.reshape(B, C, 2, STRIPS, ROWS, P).transpose(0, 1, 2, 4, 3, 5).reshape(B, C, H, W)
```

```python
import math
from contextlib import ExitStack

import numpy as np

import concourse.bass as bass
from concourse import mybir

ALU = mybir.AluOpType
ACT = mybir.ActivationFunctionType
AX = mybir.AxisListType
F32 = mybir.dt.float32

B, C, H, W = 4, 96, 32, 32
PIX = H * W
HEADS = 8
HD = C // HEADS
GROUP = C // 32
EPS = 1e-5
L2_EPS = 1e-12
P = 8
FREQ = P * P
HALF = PIX // 2
STRIP = 128
STRIPS = HALF // STRIP
GATED = C // 2
GELU_AT = 64
LANES = GELU_AT + GATED
TAPS = 9
PE_TAPS = (2, 2, 3, 3)
PARTS = (1, 1, 1, 2)
PW = W + 2
ROWS = H // 2
MASKED = -1e30


def frequencies():
    own = [(0, 0), (0, 4), (4, 0), (4, 4)]
    pairs = [(ky, kx) for kx in (1, 2, 3) for ky in range(P)] + [(ky, kx) for kx in (0, 4) for ky in (1, 2, 3)]
    return own, pairs


def basis():
    own, pairs = frequencies()
    y, x = np.meshgrid(np.arange(P), np.arange(P), indexing="ij")
    waves, back = [], []
    for ky, kx in own:
        waves.append(np.cos(2 * math.pi * (ky * y + kx * x) / P))
        back.append(1 / FREQ)
    for ky, kx in pairs:
        for wave in (np.cos, np.sin):
            waves.append(wave(2 * math.pi * (ky * y + kx * x) / P))
            back.append(2 / FREQ)
    return np.stack([w.ravel() for w in waves], 1), np.array(back)


def both_patches(block):
    out = np.zeros((2 * FREQ, 2 * FREQ), np.float32)
    out[:FREQ, :FREQ] = block
    out[FREQ:, FREQ:] = block
    return out


def filter_selection():
    own, pairs = frequencies()
    keys = own + [k for k in pairs for _ in range(2)]
    out = np.zeros((P * (P // 2 + 1), 2 * FREQ), np.float32)
    for f, (ky, kx) in enumerate(keys):
        for row in {ky, (-ky) % P} if kx in (0, 4) else {ky}:
            share = 0.5 if kx in (0, 4) and ky not in (0, 4) else 1.0
            out[row * (P // 2 + 1) + kx, f] = out[row * (P // 2 + 1) + kx, FREQ + f] = share
    return out


K_IDENT, K_GROUP, K_MASK, K_DFT, K_BACK, K_SEL = 0, 112, 208, 304, 432, 560
K_EARLY = 208
K_ALL = 688


def constants():
    waves, back = basis()
    out = np.zeros((128, K_ALL), np.float32)
    out[:LANES, K_IDENT:K_IDENT + LANES] = np.eye(LANES)
    out[:C, K_GROUP:K_GROUP + C] = np.kron(np.eye(C // GROUP), np.full((GROUP, GROUP), 1 / GROUP))
    out[:C, K_MASK:K_MASK + C] = MASKED * (1 - np.kron(np.eye(HEADS), np.ones((HD, HD))))
    out[:, K_DFT:K_DFT + 128] = both_patches(waves)
    out[:, K_BACK:K_BACK + 128] = both_patches((waves * back).T)
    out[:P * (P // 2 + 1), K_SEL:K_SEL + 128] = filter_selection()
    return out


def unit_spectrum():
    out = np.zeros((1, B * PIX), np.float32)
    out[0, ::FREQ] = FREQ
    return out


def steps(text):
    return [(w.split(".")[0], *map(int, w.split(".")[1:])) for w in text.split()]


PE_ORDER = steps("""
    stats.0 stats.1 turn.0.0 turn.0.1 setup.0 stats.2 turn.1.0 turn.1.1 gram.0 gram.1 project.0 turn.2.0
    project.1 logits.0 turn.2.1 logits.1 stats.3 spec.0.0 softmax.0 gram.2 softmax.1 spec.0.1 attend.0
    turn.3.0 mix.0 attend.1 turn.3.1 second.0 mix.1 spec.1.0 square.0 second.1 spec.1.1 group.0 square.1
    gram.3 group.1 fold.0 spec.2.0 project.2 filter.0.0 logits.2 fold.1 filter.0.1 project.3 back.0.0
    back.0.1 logits.3 softmax.2 filter.1.0 filter.1.1 softmax.3 conv.0.0 attend.2 conv.0.1 mix.2
    spec.2.1 back.1.0 second.2 attend.3 back.1.1 square.2 spec.3.0 conv.1.0 group.2 spec.3.1 mix.3
    conv.1.1 fold.2 second.3 filter.2.0 filter.2.1 square.3 back.2.0 group.3 back.2.1 conv.2.0 conv.2.1
    fold.3 final.0.0 filter.3.0 filter.3.1 back.3.0 back.3.1 conv.3.0 conv.3.1 final.0.1 final.1.0
    final.1.1 final.2.0 final.2.1 final.3.0 final.3.1
""")
ACT_ORDER = steps("""
    norm.0 norm.1 turn.0.0 turn.0.1 turn.1.0 turn.1.1 norm.2 turn.2.0 turn.2.1 spec.0.0 softmax.0 norm.3
    softmax.1 spec.0.1 turn.3.0 turn.3.1 spec.1.0 spec.1.1 spec.2.0 back.0.0 back.0.1 softmax.2
    softmax.3 spec.2.1 back.1.0 back.1.1 spec.3.0 spec.3.1 gelu.0.0 gelu.0.1 back.2.0 back.2.1 gelu.1.0
    gelu.1.1 final.0.0 back.3.0 back.3.1 gelu.2.0 gelu.2.1 final.0.1 final.1.0 gelu.3.0 final.1.1
    final.2.0 final.2.1 gelu.3.1 final.3.0 final.3.1
""")
DVE_ORDER = steps("""
    half.0 stats.0 half.1 var.0 stats.1 norm.0 var.1 half.2 norm.1 half.3 stats.2 stats.3 var.2 setup.0
    norm.2 gram.0 gram.1 project.0 project.1 logits.0 logits.1 scale.0 var.3 scale.1 softmax.0 norm.3
    attend.0 softmax.1 gram.2 q1.0 attend.1 mix.0 q1.1 second.0 mix.1 square.0 second.1 group.0 square.1
    weigh.0 gram.3 group.1 fold.0 weigh.1 project.2 filter.0.0 fold.1 logits.2 filter.0.1 scale.2
    project.3 logits.3 softmax.2 scale.3 filter.1.0 attend.2 filter.1.1 softmax.3 q1.2 attend.3
    tap.0.2.0 mix.2 tap.0.3.0 second.2 tap.0.4.0 square.2 q1.3 tap.0.5.0 group.2 tap.0.6.0 mix.3 weigh.2
    tap.0.7.0 fold.2 second.3 tap.0.8.0 filter.2.0 tap.1.2.0 square.3 filter.2.1 tap.1.3.0 tap.1.4.0
    group.3 tap.1.5.0 weigh.3 tap.1.6.0 gate.0.0 tap.1.7.0 fold.3 tap.1.8.0 tap.2.3.0 filter.3.0
    tap.2.4.0 filter.3.1 tap.2.5.0 gate.0.1 tap.2.6.0 gate.1.0 tap.2.7.0 gate.1.1 tap.2.8.0 tap.3.3.0
    tap.3.4.0 gate.2.0 tap.3.5.0 gate.2.1 tap.3.6.0 tap.3.7.0 tap.3.8.0 tap.3.3.1 tap.3.4.1 gate.3.0
    tap.3.5.1 tap.3.6.1 tap.3.7.1 tap.3.8.1 gate.3.1
""")
A_STEPS = [s for s in PE_ORDER if s[0] in ("turn", "spec", "back", "final")]
V_STEPS = [s for s in PE_ORDER if s[0] == "filter"]
TAP_STEPS = [s for s in DVE_ORDER if s[0] == "tap"]
CONV_STEPS = [s for s in PE_ORDER if s[0] == "conv"]
GELU_STEPS = [s for s in ACT_ORDER if s[0] == "gelu"]
GATE_STEPS = [s for s in DVE_ORDER if s[0] == "gate"]


def last_tap(b, h, t=TAPS - 1):
    return ("tap", b, t, h if PARTS[b] == 2 else 0)


def through(steps, step):
    return steps.index(step) + 1


def build(nc, x, wqkT, wv, projT, proj_b, temp, filt, w_inT, w_outT, w_dw, consts, unit, out):
    with ExitStack() as ctx:
        def sb(name, shape):
            return ctx.enter_context(nc.sbuf_tensor(name, shape, F32))

        def sem(name):
            return ctx.enter_context(nc.semaphore(name))

        X = sb("X", [C, B, PIX])
        XN = sb("XN", [C, B, PIX])
        XNT = sb("XNT", [STRIP, B, 2 * STRIPS, C])
        XF = sb("XF", [C + 1, B, PIX])
        Z = sb("Z", [STRIP, B, 2 * STRIPS, LANES])
        PAD = sb("PAD", [LANES, B, H + 2, PW])
        ACC = sb("ACC", [LANES, B, PIX])
        GE = sb("GE", [GATED, B, PIX])
        GT = sb("GT", [GATED, B, PIX])

        CST = sb("CST", [128, K_ALL])
        WQK = sb("WQK", [C, 2 * C])
        WV = sb("WV", [C, C])
        PRJ = sb("PRJ", [C, C])
        WIN = sb("WIN", [C, C])
        WOUT = sb("WOUT", [GATED, C])
        FLT = sb("FLT", [P * (P // 2 + 1), C])
        FREAL = sb("FREAL", [2 * FREQ, C])
        DW = sb("DW", [LANES, TAPS])
        DIAG = sb("DIAG", [LANES, max(PE_TAPS), LANES])
        PB = sb("PB", [C, 1])
        TEMP = sb("TEMP", [C, 1])
        ONES = sb("ONES", [C, 1])
        MEANW = sb("MEANW", [C, 1])
        POWER = sb("POWER", [C, 2])
        WARM = sb("WARM", [1, 2])

        BN = sb("BN", [C, B, 2, 6])
        MV = sb("MV", [C, B, 2])
        SG = sb("SG", [C, B, 1])
        ST = sb("ST", [C, B, 16])
        NEGVAR, VAR, RSTD, STD, SHIFT, MEANXN, BIAS, RQ, NMAX, SUM, RSUM, TT, NV2, V2E, R2 = (
            range(15))
        G = sb("G", [C, B, C])
        TK = sb("TK", [C, B, C])
        QQ = sb("QQ", [C, B, 2 * C])
        NRM = sb("NRM", [C, B, 2])
        RN = sb("RN", [C, B, 2])
        KL = sb("KL", [C, B, C])
        LM = sb("LM", [C, B, C])
        PR = sb("PR", [C, B, C])
        PJ = sb("PJ", [C, B, C])
        Q1 = sb("Q1", [C, B, C])
        A = sb("A", [C, B, C + 1])
        AT = sb("AT", [C, B, C])
        AGA = sb("AGA", [C, B, C])
        S2 = sb("S2", [C, B, 2])
        WI = sb("WI", [C, B, C])
        BT = sb("BT", [C + 1, B, C])

        def col(b, which):
            return ST[:, b, which:which + 1]

        CH = [ctx.enter_context(nc.psum_tensor(f"CH{i}", [128, 512], F32)) for i in range(2)]
        AB = [ctx.enter_context(nc.psum_tensor(f"AB{i}", [128, 512], F32)) for i in range(2)]
        VB = [ctx.enter_context(nc.psum_tensor(f"VB{i}", [128, 512], F32)) for i in range(2)]
        CV = ctx.enter_context(nc.psum_tensor("CV", [128, 2, 512], F32))

        x_in = [sem(f"x_in{b}") for b in range(B)]
        early_in, weights_in, late_in = sem("early_in"), sem("weights_in"), sem("late_in")
        pool_set = sem("pool_set")
        diag_set, filter_sum, filter_set = sem("diag_set"), sem("filter_sum"), sem("filter_set")
        v_done = sem("v_done")
        half_set, other_half_set = sem("half_set"), sem("other_half_set")
        stats_set, group_mean = sem("stats_set"), sem("group_mean")
        sg_set = sem("sg_set")
        shift_set, std_set, bias_set = sem("shift_set"), sem("std_set"), sem("bias_set")
        var_set, rstd_set, xn_set, mean_set = sem("var_set"), sem("rstd_set"), sem("xn_set"), sem("mean_set")
        gram_sum, gram_set = sem("gram_sum"), sem("gram_set")
        qk_sum, qk_set, logit_sum = sem("qk_sum"), sem("qk_set"), sem("logit_sum")
        norm_set, rnorm_set, logit_set = sem("norm_set"), sem("rnorm_set"), sem("logit_set")
        kl_set, turned_sum = sem("kl_set"), sem("turned_sum")
        rq_set = sem("rq_set")
        exp_set, attn_set = sem("exp_set"), sem("attn_set")
        q1_sum, q1_set, m_sum, a_set = sem("q1_sum"), sem("q1_set"), sem("m_sum"), sem("a_set")
        ag_sum, aga_set, square_sum, s2_set = sem("ag_sum"), sem("aga_set"), sem("square_sum"), sem("s2_set")
        group2_sum, var2_set, rstd2_set, wi_set = sem("group2_sum"), sem("var2_set"), sem("rstd2_set"), sem("wi_set")
        column_set = sem("column_set")
        bt_sum, bt_set = sem("bt_sum"), sem("bt_set")
        a_full, a_free = sem("a_full"), sem("a_free")
        v_full, v_free = sem("v_full"), sem("v_free")
        conv_sum, tap_set = sem("conv_sum"), sem("tap_set")
        gelu_set, gate_set = sem("gelu_set"), sem("gate_set")
        stored = sem("stored")

        block = ctx.enter_context(nc.Block())

        @block.sync
        def _(sp):
            sp.dma_start(X[:, 0, :], x[0]).then_inc(x_in[0], 16)
            sp.dma_start(CST[:, 0:K_EARLY], consts[:, 0:K_EARLY]).then_inc(early_in, 16)
            for b in range(1, B):
                sp.dma_start(X[:, b, :], x[b]).then_inc(x_in[b], 16)
            for step in ACT_ORDER:
                if step[0] == "final":
                    _, b, h = step
                    sp.wait_ge(a_free, through(A_STEPS, step))
                    sp.dma_start(out[b][:, HALF * h:HALF * (h + 1)],
                                 X[:, b, HALF * h:HALF * (h + 1)]).then_inc(stored, 16)
            sp.wait_ge(stored, 16 * 2 * B)

        @block.gpsimd
        def _(pool):
            nc.gpsimd.memset(POWER[:], -0.5).then_inc(pool_set, 1)
            nc.gpsimd.memset(ONES[:], 1.0).then_inc(pool_set, 1)
            nc.gpsimd.memset(MEANW[:], 1.0 / PIX).then_inc(pool_set, 1)
            nc.gpsimd.memset(Z[:, :, :, GATED:GELU_AT].rearrange("p b s z -> p (b s) z"),
                             0.0).then_inc(pool_set, 1)
            nc.gpsimd.memset(PAD[:, :, 0::H + 1, :], 0.0).then_inc(pool_set, 1)
            nc.gpsimd.memset(PAD[:, :, 1:H + 1, 0::PW - 1], 0.0).then_inc(pool_set, 1)
            pool.wait_ge(pool_set, 2)
            nc.gpsimd.tensor_tensor(WARM[:, 1:2], ONES[0:1, 0:1], POWER[0:1, 0:1], ALU.pow)
            for step in DVE_ORDER:
                b = step[1]
                if step[0] == "var":
                    pool.wait_ge(var_set, b + 1)
                    nc.gpsimd.tensor_tensor(col(b, RSTD), col(b, VAR), POWER[:, 0:1], ALU.pow).then_inc(rstd_set, 1)
                elif step[0] == "logits":
                    pool.wait_ge(norm_set, b + 1)
                    nc.gpsimd.tensor_tensor(RN[:, b, :], NRM[:, b, :], POWER[:], ALU.pow).then_inc(rnorm_set, 1)
                elif step[0] == "group":
                    pool.wait_ge(var2_set, b + 1)
                    nc.gpsimd.tensor_tensor(col(b, R2), col(b, V2E), POWER[:, 0:1], ALU.pow).then_inc(rstd2_set, 1)

        @block.scalar
        def _(act):
            act.dma_start(WQK[:], wqkT).then_inc(weights_in, 16)
            act.dma_start(WV[:], wv).then_inc(weights_in, 16)
            act.dma_start(PRJ[:], projT).then_inc(weights_in, 16)
            act.dma_start(PB[:], proj_b).then_inc(weights_in, 16)
            act.dma_start(TEMP[:], temp).then_inc(weights_in, 16)
            act.dma_start(WIN[:], w_inT).then_inc(weights_in, 16)
            act.dma_start(CST[:, K_EARLY:K_ALL], consts[:, K_EARLY:K_ALL]).then_inc(late_in, 16)
            act.dma_start(FLT[:], filt).then_inc(late_in, 16)
            act.dma_start(DW[:], w_dw).then_inc(late_in, 16)
            act.dma_start(WOUT[:], w_outT).then_inc(late_in, 16)
            act.dma_start(XF[C:C + 1, :, :].rearrange("p b n -> p (b n)"), unit).then_inc(late_in, 16)
            act.wait_ge(pool_set, 1)
            nc.scalar.activation(WARM[:, 0:1], POWER[0:1, 0:1], ACT.Exp)
            n = 0
            for step in ACT_ORDER:
                b = step[1]
                if step[0] in ("turn", "spec", "back", "final"):
                    h = step[2]
                    bank = AB[n % 2]
                    n += 1
                    act.wait_ge(a_full, n)
                    bias, func = 0.0, ACT.Copy
                    if step[0] == "turn":
                        dst = XNT[:, b, STRIPS * h:STRIPS * (h + 1), :]
                        src = bank[:, 0:STRIPS * C].rearrange("p (s c) -> p s c", c=C)
                    elif step[0] == "spec":
                        dst, src = XF[0:C, b, HALF * h:HALF * (h + 1)], bank[0:C, :]
                    elif step[0] == "back":
                        if b == 0 and h == 0:
                            act.wait_ge(pool_set, 6)
                        dst = PAD[:, b, 1 + ROWS * h:1 + ROWS * (h + 1), 1:1 + W]
                        src = bank[0:LANES, :].rearrange("c (y x) -> c y x", x=W)
                    else:
                        dst, src = X[:, b, HALF * h:HALF * (h + 1)], bank[0:C, :]
                        bias, func = col(b, BIAS), ACT.Identity
                    nc.scalar.activation(dst, src, func, bias=bias).then_inc(a_free, 1)
                elif step[0] == "norm":
                    act.wait_ge(shift_set, b + 1)
                    nc.scalar.activation(XN[:, b, :], X[:, b, :], ACT.Identity, bias=col(b, SHIFT),
                                         scale=col(b, RSTD)).then_inc(xn_set, 1)
                elif step[0] == "softmax":
                    act.wait_ge(logit_set, b + 1)
                    nc.scalar.activation(PR[:, b, :], LM[:, b, :], ACT.Exp, bias=col(b, NMAX),
                                         accum_out=col(b, SUM)).then_inc(exp_set, 1)
                elif step[0] == "gelu":
                    h = step[2]
                    act.wait_ge(tap_set, through(TAP_STEPS, last_tap(b, h)))
                    part = slice(HALF * h, HALF * (h + 1))
                    nc.scalar.activation(GE[:, b, part], ACC[GELU_AT:LANES, b, part], ACT.Gelu).then_inc(gelu_set, 1)

        @block.vector
        def _(dve):
            done = [0]

            def then(ins):
                done[0] += 1
                ins.then_inc(v_done, 1)
                dve.wait_ge(v_done, done[0])

            v = nc.vector
            for step in DVE_ORDER:
                name, b = step[0], step[1]
                ps = CH[b % 2]
                if name == "half":
                    dve.wait_ge(x_in[b], 16)
                    v.bn_stats(BN[:, b, 0, :], X[:, b, 0:HALF]).then_inc(half_set, 1)
                elif name == "stats":
                    v.bn_stats(BN[:, b, 1, :], X[:, b, HALF:PIX]).then_inc(other_half_set, 1)
                    dve.wait_ge(half_set, b + 1)
                    dve.wait_ge(other_half_set, b + 1)
                    then(v.bn_aggr(MV[:, b, :], BN[:, b, :, :].rearrange("p h s -> p (h s)")))
                    v.scalar_tensor_tensor(MV[:, b, 1:2], MV[:, b, 0:1], MV[:, b, 0:1], MV[:, b, 1:2],
                                           ALU.mult, ALU.add).then_inc(stats_set, 1)
                elif name == "var":
                    dve.wait_ge(group_mean, b + 1)
                    mean, square = CV[0:C, 1, 2 * b:2 * b + 1], CV[0:C, 1, 2 * b + 1:2 * b + 2]
                    then(v.tensor_scalar(col(b, NEGVAR), mean, mean, square, ALU.mult, ALU.subtract))
                    v.tensor_scalar(col(b, VAR), col(b, NEGVAR), -1.0, EPS, ALU.mult, ALU.add).then_inc(var_set, 1)
                    v.tensor_copy(SG[:, b, 0:1], mean).then_inc(sg_set, 1)
                elif name == "norm":
                    dve.wait_ge(sg_set, b + 1)
                    dve.wait_ge(rstd_set, b + 1)
                    v.scalar_tensor_tensor(col(b, SHIFT), SG[:, b, 0:1], -1.0, col(b, RSTD),
                                           ALU.mult, ALU.mult).then_inc(shift_set, 1)
                    dve.wait_ge(shift_set, b + 1)
                    v.tensor_scalar(col(b, MEANXN), MV[:, b, 0:1], col(b, RSTD), col(b, SHIFT),
                                    ALU.mult, ALU.add).then_inc(mean_set, 1)
                    v.tensor_tensor(col(b, STD), col(b, VAR), col(b, RSTD), ALU.mult).then_inc(std_set, 1)
                elif name == "setup":
                    dve.wait_ge(filter_sum, 1)
                    v.tensor_copy(FREAL[:], VB[0][:, 0:C]).then_inc(filter_set, 1)
                    dve.wait_ge(late_in, 16 * 5)
                    for t in range(max(PE_TAPS)):
                        v.tensor_scalar(DIAG[:, t, :], CST[0:LANES, K_IDENT:K_IDENT + LANES], DW[:, t:t + 1],
                                        None, ALU.mult).then_inc(diag_set, 1)
                elif name == "gram":
                    dve.wait_ge(gram_sum, b + 1)
                    v.tensor_copy(G[:, b, :], CV[0:C, 0, 0:C]).then_inc(gram_set, 1)
                    if b == 0:
                        dve.wait_ge(weights_in, 16 * 6)
                    v.tensor_tensor(col(b, BIAS), SG[:, b, 0:1], PB[:], ALU.add).then_inc(bias_set, 1)
                elif name == "project":
                    dve.wait_ge(qk_sum, b + 1)
                    v.tensor_copy(TK[:, b, :], ps[0:C, C:2 * C]).then_inc(qk_set, 1)
                    v.tensor_tensor(QQ[:, b, :], WQK[:], ps[0:C, 0:2 * C], ALU.mult).then_inc(qk_set, 1)
                elif name == "logits":
                    dve.wait_ge(logit_sum, b + 1)
                    v.tensor_scalar(NRM[:, b, :], ps[0:C, 384:386], L2_EPS * L2_EPS, None,
                                    ALU.max).then_inc(norm_set, 1)
                elif name == "scale":
                    dve.wait_ge(rnorm_set, b + 1)
                    v.tensor_scalar(KL[:, b, :], ps[0:C, 192:192 + C], RN[:, b, 1:2], None,
                                    ALU.mult).then_inc(kl_set, 1)
                    v.tensor_tensor(col(b, RQ), RN[:, b, 0:1], TEMP[:], ALU.mult).then_inc(rq_set, 1)
                elif name == "softmax":
                    dve.wait_ge(turned_sum, b + 1)
                    dve.wait_ge(rq_set, b + 1)
                    then(v.scalar_tensor_tensor(LM[:, b, :], ps[0:C, 288:288 + C], col(b, RQ),
                                                CST[0:C, K_MASK:K_MASK + C], ALU.mult, ALU.add))
                    v.tensor_reduce(col(b, NMAX), LM[:, b, :], AX.X, ALU.max, negate=True).then_inc(logit_set, 1)
                elif name == "attend":
                    dve.wait_ge(exp_set, b + 1)
                    then(v.reciprocal(col(b, RSUM), col(b, SUM)))
                    v.tensor_scalar(PJ[:, b, :], PRJ[:], col(b, RSUM), None, ALU.mult).then_inc(attn_set, 1)
                elif name == "q1":
                    dve.wait_ge(q1_sum, b + 1)
                    v.tensor_copy(Q1[:, b, :], ps[0:C, 0:C]).then_inc(q1_set, 1)
                elif name == "mix":
                    dve.wait_ge(m_sum, b + 1)
                    dve.wait_ge(std_set, b + 1)
                    v.scalar_tensor_tensor(AT[:, b, :], CST[0:C, K_IDENT:K_IDENT + C], col(b, STD),
                                           ps[0:C, 192:192 + C], ALU.mult, ALU.add).then_inc(a_set, 1)
                    v.scalar_tensor_tensor(A[:, b, 0:C], CST[0:C, K_IDENT:K_IDENT + C], col(b, STD),
                                           ps[0:C, 96:96 + C], ALU.mult, ALU.add).then_inc(a_set, 1)
                elif name == "second":
                    dve.wait_ge(ag_sum, b + 1)
                    v.tensor_tensor(AGA[:, b, :], AT[:, b, :], ps[0:C, 288:288 + C], ALU.mult).then_inc(aga_set, 1)
                elif name == "square":
                    dve.wait_ge(square_sum, b + 1)
                    then(v.tensor_scalar(S2[:, b, 0:1], ps[0:C, 384:385], PB[:, 0:1], None, ALU.add))
                    then(v.tensor_tensor(col(b, TT), S2[:, b, 0:1], ps[0:C, 384:385], ALU.add))
                    v.scalar_tensor_tensor(S2[:, b, 1:2], col(b, TT), PB[:, 0:1], ps[0:C, 385:386],
                                           ALU.mult, ALU.add).then_inc(s2_set, 1)
                elif name == "group":
                    dve.wait_ge(group2_sum, b + 1)
                    mean, square = ps[0:C, 480:481], ps[0:C, 481:482]
                    then(v.tensor_scalar(col(b, NV2), mean, mean, square, ALU.mult, ALU.subtract))
                    v.tensor_scalar(col(b, V2E), col(b, NV2), -1.0, EPS, ALU.mult, ALU.add).then_inc(var2_set, 1)
                    v.tensor_scalar(A[:, b, C:C + 1], mean, -1.0, PB[:, 0:1],
                                    ALU.mult, ALU.add).then_inc(column_set, 1)
                elif name == "weigh":
                    dve.wait_ge(rstd2_set, b + 1)
                    v.tensor_scalar(WI[:, b, :], WIN[:], col(b, R2), None, ALU.mult).then_inc(wi_set, 1)
                elif name == "fold":
                    dve.wait_ge(bt_sum, b + 1)
                    v.tensor_copy(BT[:, b, :], ps[0:C + 1, 0:C]).then_inc(bt_set, 1)
                elif name == "filter":
                    h, n = step[2], through(V_STEPS, step)
                    dve.wait_ge(v_full, n)
                    if b == 0 and h == 0:
                        dve.wait_ge(filter_set, 1)
                    zs = Z[:, b, STRIPS * h:STRIPS * (h + 1), :]
                    for first, at in ((0, 0), (GATED, GELU_AT)):
                        ins = v.tensor_tensor(
                            zs[:, :, at:at + GATED],
                            VB[(n - 1) % 2][:, 0:STRIPS * C].rearrange("p (s c) -> p s c", c=C)[
                                :, :, first:first + GATED],
                            FREAL[:, first:first + GATED].unsqueeze(1).broadcast_to([2 * FREQ, STRIPS, GATED]),
                            ALU.mult)
                    ins.then_inc(v_free, 1)
                elif name == "tap":
                    t, part = step[2:]
                    rows = H // PARTS[b]
                    y = rows * part
                    acc = ACC[:, b, W * y:W * (y + rows)].rearrange("c (y x) -> c y x", x=W)
                    if t == PE_TAPS[b]:
                        dve.wait_ge(conv_sum, through(CONV_STEPS, ("conv", b, part if PARTS[b] == 2 else 1)))
                        before = (CV[0:LANES, part, :] if PARTS[b] == 2 else
                                  CV[0:LANES, :, :].rearrange("c h n -> c (h n)")).rearrange(
                                      "c (y x) -> c y x", x=W)
                    else:
                        dve.wait_ge(tap_set, through(TAP_STEPS, ("tap", b, t - 1, part)))
                        before = acc
                    dy, dx = divmod(t, 3)
                    v.scalar_tensor_tensor(acc, PAD[:, b, y + dy:y + dy + rows, dx:dx + W], DW[:, t:t + 1],
                                           before, ALU.mult, ALU.add).then_inc(tap_set, 1)
                elif name == "gate":
                    h = step[2]
                    dve.wait_ge(gelu_set, through(GELU_STEPS, ("gelu", b, h)))
                    part = slice(HALF * h, HALF * (h + 1))
                    v.tensor_tensor(GT[:, b, part], GE[:, b, part], ACC[0:GATED, b, part],
                                    ALU.mult).then_inc(gate_set, 1)

        @block.tensor
        def _(pe):
            def mm(o, lhsT, rhs, start=True, stop=True):
                return nc.tensor.matmul(o, lhsT, rhs, start=start, stop=stop)

            ident = CST[0:C, K_IDENT:K_IDENT + C]
            group = CST[0:C, K_GROUP:K_GROUP + C]
            for step in PE_ORDER:
                name, b = step[0], step[1]
                ps = CH[b % 2]
                if name in ("turn", "spec", "back", "final"):
                    h, n = step[2], through(A_STEPS, step)
                    bank = AB[(n - 1) % 2]
                    if n > 2:
                        pe.wait_ge(a_free, n - 2)
                    if name == "turn":
                        pe.wait_ge(xn_set, b + 1)
                        for s in range(STRIPS):
                            at = HALF * h + STRIP * s
                            ins = nc.tensor.transpose(bank[:, C * s:C * (s + 1)], XN[:, b, at:at + STRIP], ident)
                    elif name == "spec":
                        pe.wait_ge(a_free, through(A_STEPS, ("turn", b, h)))
                        if b == 0 and h == 0:
                            pe.wait_ge(late_in, 16 * 5)
                        for s in range(STRIPS):
                            ins = mm(bank[0:C, STRIP * s:STRIP * (s + 1)], XNT[:, b, STRIPS * h + s, :],
                                     CST[:, K_DFT:K_DFT + 128])
                    elif name == "back":
                        pe.wait_ge(v_free, through(V_STEPS, ("filter", b, h)))
                        if b == 0 and h == 0:
                            pe.wait_ge(pool_set, 4)
                        rows = bank[0:LANES, :].rearrange("c (y s x) -> c s y x", s=STRIPS, x=P)
                        for s in range(STRIPS):
                            ins = mm(rows[:, s], Z[:, b, STRIPS * h + s, :], CST[:, K_BACK:K_BACK + 128])
                    else:
                        if b == 0 and h == 0:
                            pe.wait_ge(bias_set, B)
                        mm(bank[0:C, :], AT[:, b, :], XN[:, b, HALF * h:HALF * (h + 1)], stop=False)
                        pe.wait_ge(gate_set, through(GATE_STEPS, ("gate", b, h)))
                        ins = mm(bank[0:C, :], WOUT[:],
                                 GT[:, b, :].rearrange("p (h y s x) -> p h s y x", h=2, y=ROWS, x=P)[:, h],
                                 start=False)
                    ins.then_inc(a_full, 1)
                elif name == "stats":
                    pe.wait_ge(stats_set, b + 1)
                    if b == 0:
                        pe.wait_ge(early_in, 16)
                    mm(CV[0:C, 1, 2 * b:2 * b + 2], group, MV[:, b, :]).then_inc(group_mean, 1)
                elif name == "gram":
                    pe.wait_ge(a_free, through(A_STEPS, ("turn", b, 1)))
                    if b:
                        pe.wait_ge(gram_set, b)
                    for s in range(2 * STRIPS):
                        ins = mm(CV[0:C, 0, 0:C], XNT[:, b, s, :], XNT[:, b, s, :], start=(s == 0),
                                 stop=(s == 2 * STRIPS - 1))
                    ins.then_inc(gram_sum, 1)
                elif name == "setup":
                    pe.wait_ge(late_in, 16 * 5)
                    mm(VB[0][:, 0:C], CST[0:P * (P // 2 + 1), K_SEL:K_SEL + 128], FLT[:]).then_inc(filter_sum, 1)
                elif name == "project":
                    pe.wait_ge(gram_set, b + 1)
                    if b == 0:
                        pe.wait_ge(weights_in, 16 * 6)
                        pe.wait_ge(pool_set, 3)
                    if b >= 2:
                        pe.wait_ge(bt_set, b - 1)
                    mm(ps[0:C, 0:2 * C], G[:, b, :], WQK[:]).then_inc(qk_sum, 1)
                elif name == "logits":
                    pe.wait_ge(qk_set, 2 * (b + 1))
                    mm(ps[0:C, 384:385], QQ[:, b, 0:C], ONES[:])
                    mm(ps[0:C, 385:386], QQ[:, b, C:2 * C], ONES[:])
                    mm(ps[0:C, 192:192 + C], TK[:, b, :], WQK[:, 0:C]).then_inc(logit_sum, 1)
                elif name == "softmax":
                    pe.wait_ge(kl_set, b + 1)
                    mm(ps[0:C, 288:288 + C], KL[:, b, :], ident).then_inc(turned_sum, 1)
                elif name == "attend":
                    pe.wait_ge(attn_set, b + 1)
                    mm(ps[0:C, 0:C], PR[:, b, :], PJ[:, b, :]).then_inc(q1_sum, 1)
                elif name == "mix":
                    pe.wait_ge(q1_set, b + 1)
                    mm(ps[0:C, 192:192 + C], WV[:], Q1[:, b, :])
                    mm(ps[0:C, 96:96 + C], Q1[:, b, :], WV[:]).then_inc(m_sum, 1)
                elif name == "second":
                    pe.wait_ge(a_set, 2 * (b + 1))
                    pe.wait_ge(mean_set, b + 1)
                    mm(ps[0:C, 384:385], AT[:, b, :], col(b, MEANXN))
                    mm(ps[0:C, 288:288 + C], G[:, b, :], AT[:, b, :]).then_inc(ag_sum, 1)
                elif name == "square":
                    pe.wait_ge(aga_set, b + 1)
                    mm(ps[0:C, 385:386], AGA[:, b, :], MEANW[:]).then_inc(square_sum, 1)
                elif name == "group":
                    pe.wait_ge(s2_set, b + 1)
                    mm(ps[0:C, 480:482], group, S2[:, b, :]).then_inc(group2_sum, 1)
                elif name == "fold":
                    pe.wait_ge(column_set, b + 1)
                    pe.wait_ge(wi_set, b + 1)
                    mm(ps[0:C + 1, 0:C], A[:, b, :], WI[:, b, :]).then_inc(bt_sum, 1)
                elif name == "filter":
                    h, n = step[2], through(V_STEPS, step)
                    pe.wait_ge(bt_set, b + 1)
                    pe.wait_ge(a_free, through(A_STEPS, ("spec", b, h)))
                    pe.wait_ge(filter_set, 1)
                    if n > 2:
                        pe.wait_ge(v_free, n - 2)
                    for s in range(STRIPS):
                        at = HALF * h + STRIP * s
                        ins = mm(VB[(n - 1) % 2][:, C * s:C * (s + 1)], XF[:, b, at:at + STRIP], BT[:, b, :])
                    ins.then_inc(v_full, 1)
                elif name == "conv":
                    h = step[2]
                    pe.wait_ge(a_free, through(A_STEPS, ("back", b, 1)))
                    if b == 0:
                        pe.wait_ge(gram_set, B)
                        pe.wait_ge(sg_set, B)
                        pe.wait_ge(diag_set, max(PE_TAPS))
                    else:
                        pe.wait_ge(tap_set, through(TAP_STEPS, last_tap(b - 1, h, PE_TAPS[b - 1])))
                    for t in range(PE_TAPS[b]):
                        dy, dx = divmod(t, 3)
                        ins = mm(CV[0:LANES, h, :], DIAG[:, t, :],
                                 PAD[:, b, ROWS * h + dy:ROWS * (h + 1) + dy, dx:dx + W],
                                 start=(t == 0), stop=(t == PE_TAPS[b] - 1))
                    ins.then_inc(conv_sum, 1)



def kernel(**inputs):
    import concourse.bacc as bacc
    from concourse.bass_utils import run_bass_kernel_spmd

    f32 = np.float32
    qkv = np.asarray(inputs["L0_conv_qkv_w"])
    w_out = np.asarray(inputs["L1_conv_w_out"])
    gates_first = np.r_[GATED:C, 0:GATED]
    dw = np.zeros((LANES, TAPS), f32)
    dw[:GATED] = np.asarray(inputs["L1_conv_w_dw"]).reshape(C, TAPS)[GATED:]
    dw[GELU_AT:] = np.asarray(inputs["L1_conv_w_dw"]).reshape(C, TAPS)[:GATED]
    x = np.asarray(inputs["x"]).reshape(B, C, 2, ROWS, STRIPS, P).transpose(0, 1, 2, 4, 3, 5)
    arrays = {
        "x": x.reshape(B, C, PIX),
        "wqkT": qkv[:2 * C].T,
        "wv": qkv[2 * C:],
        "projT": np.asarray(inputs["L0_conv_proj_w"]).T,
        "proj_b": np.asarray(inputs["L0_conv_proj_b"]).reshape(C, 1),
        "temp": np.repeat(np.asarray(inputs["L0_conv_temperature"]).reshape(HEADS), HD).reshape(C, 1),
        "filt": np.asarray(inputs["L1_conv_fft_filter"]).reshape(C, P * (P // 2 + 1)).T[:, gates_first],
        "w_inT": np.asarray(inputs["L1_conv_w_in"]).T[:, gates_first],
        "w_outT": w_out.T,
        "w_dw": dw,
        "consts": constants(),
        "unit": unit_spectrum(),
    }
    arrays = {f"in_{k}": np.ascontiguousarray(v) for k, v in arrays.items()}
    nc = bacc.Bacc("TRN2", target_bir_lowering=False, num_devices=1)
    args = [nc.dram_tensor(k, v.shape, mybir.dt.from_np(v.dtype), kind="ExternalInput").ap()
            for k, v in arrays.items()]
    out = nc.dram_tensor("out", [B, C, PIX], F32, kind="ExternalOutput").ap()
    build(nc, *args, out)
    r = run_bass_kernel_spmd(nc, [arrays], core_ids=[0])
    got = np.asarray(r.results[0]["out"])
    return got.reshape(B, C, 2, STRIPS, ROWS, P).transpose(0, 1, 2, 4, 3, 5).reshape(B, C, H, W)
```

```python
import math
from contextlib import ExitStack

import numpy as np

import concourse.bass as bass
from concourse import mybir

ALU = mybir.AluOpType
ACT = mybir.ActivationFunctionType
AX = mybir.AxisListType
F32 = mybir.dt.float32

B, C, H, W = 4, 96, 32, 32
PIX = H * W
C1 = C + 1
HEADS = 8
HD = C // HEADS
GROUP = C // 32
EPS = 1e-5
L2_EPS = 1e-12
P = 8
FREQ = P * P
HALF = PIX // 2
STRIP = 128
STRIPS = HALF // STRIP
GATED = C // 2
GELU_AT = 64
LANES = GELU_AT + GATED
TAPS = 9
PE_TAPS = (0, 0, 0, 5)
POOL_TAPS = (2, 2, 2, 0)
POOL_FIRST = (0, 0, 0, 0)
POOL_GATES = 3
PARTS = (1, 1, 2, 2)
PW = W + 2
ROWS = H // 2
MASKED = -1e30


def frequencies():
    own = [(0, 0), (0, 4), (4, 0), (4, 4)]
    pairs = [(ky, kx) for kx in (1, 2, 3) for ky in range(P)] + [(ky, kx) for kx in (0, 4) for ky in (1, 2, 3)]
    return own, pairs


def basis():
    own, pairs = frequencies()
    y, x = np.meshgrid(np.arange(P), np.arange(P), indexing="ij")
    waves, back = [], []
    for ky, kx in own:
        waves.append(np.cos(2 * math.pi * (ky * y + kx * x) / P))
        back.append(1 / FREQ)
    for ky, kx in pairs:
        for wave in (np.cos, np.sin):
            waves.append(wave(2 * math.pi * (ky * y + kx * x) / P))
            back.append(2 / FREQ)
    return np.stack([w.ravel() for w in waves], 1), np.array(back)


def both_patches(block):
    out = np.zeros((2 * FREQ, 2 * FREQ), np.float32)
    out[:FREQ, :FREQ] = block
    out[FREQ:, FREQ:] = block
    return out


def filter_selection():
    own, pairs = frequencies()
    keys = own + [k for k in pairs for _ in range(2)]
    out = np.zeros((P * (P // 2 + 1), 2 * FREQ), np.float32)
    for f, (ky, kx) in enumerate(keys):
        for row in {ky, (-ky) % P} if kx in (0, 4) else {ky}:
            share = 0.5 if kx in (0, 4) and ky not in (0, 4) else 1.0
            out[row * (P // 2 + 1) + kx, f] = out[row * (P // 2 + 1) + kx, FREQ + f] = share
    return out


K_GROUP, K_DFT, K_IDENT = 0, C, C + 2 * FREQ
K_EARLY = K_MASK = K_IDENT + LANES
K_BACK, K_SEL = K_MASK + C, K_MASK + C + 2 * FREQ
K_ALL = K_SEL + 2 * FREQ
W_QK, W_V, W_VT, W_PROJ, W_IN, W_IDENT = (i * C for i in (0, 2, 3, 4, 5, 6))
W_BIAS, W_TEMP = 7 * C, 7 * C + 1
W_ALL = 7 * C + 2
L_FILTER, L_OUT, L_DW = 0, C, 2 * C
L_ALL = L_DW + TAPS


def constants():
    waves, back = basis()
    out = np.zeros((128, K_ALL), np.float32)
    out[:LANES, K_IDENT:K_IDENT + LANES] = np.eye(LANES)
    out[:C, K_GROUP:K_GROUP + C] = np.kron(np.eye(C // GROUP), np.full((GROUP, GROUP), 1 / (GROUP * PIX)))
    out[:C, K_MASK:K_MASK + C] = MASKED * (1 - np.kron(np.eye(HEADS), np.ones((HD, HD))))
    out[:, K_DFT:K_DFT + 2 * FREQ] = both_patches(waves)
    out[:, K_BACK:K_BACK + 2 * FREQ] = both_patches((waves * back).T)
    out[:P * (P // 2 + 1), K_SEL:K_SEL + 2 * FREQ] = filter_selection()
    return out


def steps(text):
    return [(w.split(".")[0], *map(int, w.split(".")[1:])) for w in text.split()]


PE_ORDER = steps("""
    gram.0 gram.1 stats.0 gram.2 setup.0 stats.1 shift.0 gram.3 stats.2 project.0 shift.1 spec.0.0
    logits.0 project.1 spec.0.1 logits.1 softmax.0 shift.2 spec.1.0 stats.3 project.2 softmax.1 attend.0
    spec.1.1 mix.0 shift.3 attend.1 second.0 mix.1 square.0 project.3 group.0 logits.2 second.1 spec.2.0
    fold.0 logits.3 square.1 filter.0.0 group.1 softmax.2 spec.2.1 softmax.3 filter.0.1 back.0.0
    attend.2 fold.1 back.0.1 filter.1.0 mix.2 attend.3 second.2 filter.1.1 square.2 group.2 spec.3.0
    back.1.0 spec.3.1 fold.2 mix.3 back.1.1 filter.2.0 second.3 filter.2.1 square.3 base.0.0 group.3
    back.2.0 fold.3 base.0.1 filter.3.0 filter.3.1 back.2.1 back.3.0 base.1.0 back.3.1 final.0.0
    final.0.1 conv.3.0 base.1.1 conv.3.1 base.2.0 final.1.0 final.1.1 base.2.1 base.3.0 base.3.1
    final.2.0 final.2.1 final.3.0 final.3.1
""")
ACT_ORDER = steps("""
    shift.0 shift.1 spec.0.0 shift.2 softmax.0 spec.0.1 q1.0 softmax.1 q1.1 shift.3 spec.1.0 square.0
    square.1 spec.1.1 spec.2.0 softmax.2 spec.2.1 back.0.0 q1.2 softmax.3 back.0.1 tap.0.0.0 square.2
    tap.0.8.0 spec.3.0 q1.3 back.1.0 spec.3.1 tap.0.7.0 back.1.1 tap.1.0.0 square.3 tap.1.7.0 back.2.0
    gelu.0.0 back.2.1 gelu.0.1 tap.2.0.0 back.3.0 back.3.1 tap.2.8.1 final.0.0 tap.1.8.0 tap.2.7.0
    tap.2.7.1 tap.2.0.1 gelu.1.0 tap.2.8.0 final.0.1 gelu.1.1 gelu.2.0 final.1.0 final.1.1 gelu.2.1
    gelu.3.0 gelu.3.1 final.2.0 final.2.1 final.3.0 final.3.1
""")
DVE_ORDER = steps("""
    gram.0 var.0 gram.1 norm.0 var.1 gram.2 norm.1 var.2 project.0 setup.0 logits.0 norm.2 project.1
    scale.0 gram.3 logits.1 softmax.0 scale.1 attend.0 var.3 softmax.1 norm.3 attend.1 mix.0 project.2
    second.0 mix.1 group.0 project.3 logits.2 weigh.0 second.1 fold.0 logits.3 scale.2 scale.3 group.1
    softmax.2 filter.0.0 attend.2 weigh.1 filter.0.1 softmax.3 fold.1 attend.3 filter.1.0 mix.2
    tap.0.1.0 second.2 tap.0.2.0 group.2 tap.0.3.0 weigh.2 filter.1.1 tap.0.4.0 fold.2 mix.3 tap.0.5.0
    second.3 tap.0.6.0 filter.2.0 group.3 filter.2.1 weigh.3 tap.1.1.0 fold.3 tap.1.2.0 filter.3.0
    tap.1.3.0 filter.3.1 tap.1.4.0 tap.1.5.0 tap.1.6.0 tap.2.1.0 tap.2.2.0 tap.2.3.0 tap.2.4.0 tap.2.5.0
    tap.2.6.0 tap.2.1.1 tap.3.5.0 tap.2.2.1 tap.2.3.1 tap.2.4.1 tap.2.5.1 tap.2.6.1 tap.3.5.1 tap.3.6.0
    tap.3.6.1 tap.3.7.0 tap.3.7.1 tap.3.8.0 tap.3.8.1 gate.3.0 gate.3.1
""")
POOL_ORDER = steps("""
    var.0 var.1 var.2 logits.0 logits.1 var.3 group.0 logits.2 logits.3 group.1 group.2 group.3
    tap.0.7.0 tap.0.8.0 gate.0.0 gate.0.1 tap.1.7.0 tap.1.8.0 tap.2.7.0 tap.2.8.0 gate.1.0 gate.1.1
    tap.2.7.1 tap.2.8.1 gate.2.0 gate.2.1
""")
A_STEPS = [s for s in PE_ORDER if s[0] in ("spec", "back")]
V_STEPS = [s for s in PE_ORDER if s[0] == "filter"]
TAP_STEPS = [s for s in DVE_ORDER if s[0] == "tap"]
ACT_TAP_STEPS = [s for s in ACT_ORDER if s[0] == "tap"]
CONV_STEPS = [s for s in PE_ORDER if s[0] == "conv"]
GELU_STEPS = [s for s in ACT_ORDER if s[0] == "gelu"]
GATE_STEPS = [s for s in DVE_ORDER if s[0] == "gate"]


def final_number(b, h):
    return 2 * b + h


def tap_step(b, h, t):
    return ("tap", b, t, h if PARTS[b] == 2 else 0)


def tap_parts(b, part):
    rows = H // PARTS[b]
    return rows * part, rows


def pool_taps(b):
    return range(1, 1 + POOL_TAPS[b]) if POOL_FIRST[b] else range(TAPS - POOL_TAPS[b], TAPS)


def slot(b, t):
    return sum(POOL_TAPS[:b]) + t - pool_taps(b)[0]


def through(steps, step):
    return steps.index(step) + 1


def build(nc, x, xT, consts, weights, late, out):
    with ExitStack() as ctx:
        def sb(name, shape):
            return ctx.enter_context(nc.sbuf_tensor(name, shape, F32))

        def sem(name):
            return ctx.enter_context(nc.semaphore(name))

        X = sb("X", [C, B, PIX])
        XT = sb("XT", [STRIP, B, 2 * STRIPS, C1])
        XF = sb("XF", [C1, B, PIX])
        Z = sb("Z", [STRIP, B, 2 * STRIPS, LANES])
        PAD = sb("PAD", [LANES, B, H + 2, PW])
        ACC = sb("ACC", [LANES, B, PIX])
        SCALED = sb("SCALED", [LANES, max(sum(POOL_TAPS), 1), PIX])
        GE = sb("GE", [GATED, B, PIX])
        GT = sb("GT", [GATED, B, PIX])

        CST = sb("CST", [128, K_ALL])
        WTS = sb("WTS", [C1, W_ALL])
        LATE = sb("LATE", [128, L_ALL])
        FREAL = sb("FREAL", [2 * FREQ, C])
        DIAG = sb("DIAG", [LANES, max(PE_TAPS), LANES])
        ONES = sb("ONES", [C1, 1])
        POWER = sb("POWER", [C, 2])
        WARM = sb("WARM", [1, 2])

        ST = sb("ST", [C1, B, 12])
        NEGMEAN, NEGVAR, VAR, RSTD, SHIFT, BIAS, RQ, NMAX, SUM, RSUM, V2E, R2 = range(12)
        G = sb("G", [C1, B, C1 + 1])
        DUMP = sb("DUMP", [C, C])
        WA = sb("WA", [C1, B, 2 * C])
        U = sb("U", [C, B, 1])
        TK = sb("TK", [C1, B, C])
        QQ = sb("QQ", [C1, B, 2 * C])
        NRM = sb("NRM", [C, B, 2])
        RN = sb("RN", [C, B, 2])
        KL = sb("KL", [C, B, C])
        LM = sb("LM", [C, B, C])
        PR = sb("PR", [C, B, C])
        PJ = sb("PJ", [C, B, C])
        Q1 = sb("Q1", [C, B, C])
        M = sb("M", [C, B, C1])
        AT = sb("AT", [C1, B, C])
        AGA = sb("AGA", [C1, B, C])
        S2 = sb("S2", [C, B, 2])
        V2 = sb("V2", [C, B, 1])
        WI = sb("WI", [C1, B, C])
        BT = sb("BT", [C1, B, C])

        def col(b, which):
            return ST[0:C, b, which:which + 1]

        CH = [ctx.enter_context(nc.psum_tensor(f"CH{i}", [128, 512], F32)) for i in range(2)]
        AB = [ctx.enter_context(nc.psum_tensor(f"AB{i}", [128, 512], F32)) for i in range(2)]
        VB = [ctx.enter_context(nc.psum_tensor(f"VB{i}", [128, 512], F32)) for i in range(2)]
        CV = ctx.enter_context(nc.psum_tensor("CV", [128, 2, 512], F32))
        FB = [CH[0], CH[1], VB[0], VB[1]]
        SMALL = [CH[0][:, :], CH[1][:, :], CV[:, 0, :], CV[:, 1, :]]
        P_SUMS, P_U, P_GRAM = 4 * C, 4 * C + 4, 4 * C + 16
        P_GROUP = P_GRAM + C1 + 3

        x_in = [sem(f"x_in{b}") for b in range(B)]
        first_in = sem("first_in")
        xt_in = [sem(f"xt_in{b}") for b in range(B)]
        early_in, weights_in, late_in = sem("early_in"), sem("weights_in"), sem("late_in")
        pool_set = sem("pool_set")
        diag_set, filter_sum, filter_set = sem("diag_set"), sem("filter_sum"), sem("filter_set")
        v_done = sem("v_done")
        gram_sum, gram_set, diagonal_set = sem("gram_sum"), sem("gram_set"), sem("diagonal_set")
        group_mean, negmean_set = sem("group_mean"), sem("negmean_set")
        var_set, shift_set = sem("var_set"), sem("shift_set")
        scaled_set, shift_sum, wa_set, u_set = sem("scaled_set"), sem("shift_sum"), sem("wa_set"), sem("u_set")
        qk_sum, qk_set, logit_sum = sem("qk_sum"), sem("qk_set"), sem("logit_sum")
        norm_set, logit_set = sem("norm_set"), sem("logit_set")
        kl_set, turned_sum = sem("kl_set"), sem("turned_sum")
        rq_set = sem("rq_set")
        exp_set, attn_set = sem("exp_set"), sem("attn_set")
        q1_sum, q1_set, m_sum = sem("q1_sum"), sem("q1_set"), sem("m_sum")
        at_set, m_set, bias_set = sem("at_set"), sem("m_set"), sem("bias_set")
        ag_sum, aga_set, square_sum, s2_set = sem("ag_sum"), sem("aga_set"), sem("square_sum"), sem("s2_set")
        group2_sum, var2_set, wi_set = sem("group2_sum"), sem("var2_set"), sem("wi_set")
        column_set = sem("column_set")
        bt_sum, bt_set = sem("bt_sum"), sem("bt_set")
        a_full, a_free = sem("a_full"), sem("a_free")
        v_full, v_free = sem("v_full"), sem("v_free")
        f_full, f_free = sem("f_full"), sem("f_free")
        conv_sum, act_tap_set = sem("conv_sum"), sem("act_tap_set")
        tap_set, pool_done = sem("tap_set"), sem("pool_done")
        gelu_set, gate_set = sem("gelu_set"), sem("gate_set")
        stored = sem("stored")

        block = ctx.enter_context(nc.Block())

        @block.sync
        def _(sp):
            sp.dma_start(XT[:, 0, 0:STRIPS], xT[0][:, 0:STRIPS]).then_inc(first_in, 16)
            sp.dma_start(XT[:, 0, STRIPS:], xT[0][:, STRIPS:]).then_inc(xt_in[0], 16)
            for b in range(1, B):
                sp.dma_start(XT[:, b], xT[b]).then_inc(xt_in[b], 16)
            for b in range(B):
                sp.dma_start(X[:, b, :], x[b]).then_inc(x_in[b], 16)
            for step in ACT_ORDER:
                if step[0] == "final":
                    _, b, h = step
                    sp.wait_ge(f_free, final_number(b, h) + 1)
                    sp.dma_start(out[b][:, HALF * h:HALF * (h + 1)],
                                 X[:, b, HALF * h:HALF * (h + 1)]).then_inc(stored, 16)
            sp.wait_ge(stored, 16 * 2 * B)

        @block.gpsimd
        def _(pool):
            nc.gpsimd.memset(POWER[:], -0.5).then_inc(pool_set, 1)
            nc.gpsimd.memset(ONES[:], 1.0).then_inc(pool_set, 1)
            pool.wait_ge(pool_set, 2)
            nc.gpsimd.memset(ST[C:C1, :, RSTD:RSTD + 1], 1.0).then_inc(pool_set, 1)
            pool.wait_ge(pool_set, 3)
            nc.gpsimd.memset(WI[C:C1, :, :], 0.0).then_inc(pool_set, 1)
            pool.wait_ge(pool_set, 4)
            nc.gpsimd.memset(Z[:, :, :, GATED:GELU_AT].rearrange("p b s z -> p (b s) z"),
                             0.0).then_inc(pool_set, 1)
            nc.gpsimd.memset(PAD[:, :, 0::H + 1, :], 0.0).then_inc(pool_set, 1)
            nc.gpsimd.memset(PAD[:, :, 1:H + 1, 0::PW - 1], 0.0).then_inc(pool_set, 1)
            pool.wait_ge(pool_set, 2)
            nc.gpsimd.tensor_tensor(WARM[:, 1:2], ONES[0:1, 0:1], POWER[0:1, 0:1], ALU.pow)
            for n, step in enumerate(POOL_ORDER):
                b = step[1]
                if n:
                    pool.wait_ge(pool_done, n)
                else:
                    pool.wait_ge(pool_set, 7)
                if step[0] == "var":
                    pool.wait_ge(var_set, b + 1)
                    ins = nc.gpsimd.tensor_tensor(col(b, RSTD), col(b, VAR), POWER[:, 0:1], ALU.pow)
                elif step[0] == "logits":
                    pool.wait_ge(norm_set, b + 1)
                    ins = nc.gpsimd.tensor_tensor(RN[:, b, :], NRM[:, b, :], POWER[:], ALU.pow)
                elif step[0] == "group":
                    pool.wait_ge(var2_set, b + 1)
                    ins = nc.gpsimd.tensor_tensor(col(b, R2), col(b, V2E), POWER[:, 0:1], ALU.pow)
                elif step[0] == "tap":
                    t, part = step[2:]
                    if t == 1:
                        pool.wait_ge(act_tap_set, through(ACT_TAP_STEPS, ("tap", b, 0, part)))
                    elif t - 1 not in pool_taps(b):
                        pool.wait_ge(tap_set, through(TAP_STEPS, ("tap", b, t - 1, part)))
                    pool.wait_ge(act_tap_set, through(ACT_TAP_STEPS, step))
                    y, rows = tap_parts(b, part)
                    at = slice(W * y, W * (y + rows))
                    ins = nc.gpsimd.tensor_tensor(ACC[:, b, at], ACC[:, b, at], SCALED[:, slot(b, t), at], ALU.add)
                elif step[0] == "gate":
                    pool.wait_ge(gelu_set, through(GELU_STEPS, ("gelu", b, step[2])))
                    at = slice(HALF * step[2], HALF * (step[2] + 1))
                    ins = nc.gpsimd.tensor_tensor(GT[:, b, at], GE[:, b, at], ACC[0:GATED, b, at], ALU.mult)
                ins.then_inc(pool_done, 1)

        @block.scalar
        def _(act):
            act.dma_start(CST[:, 0:K_EARLY], consts[:, 0:K_EARLY]).then_inc(early_in, 16)
            act.dma_start(WTS[:], weights).then_inc(weights_in, 16)
            act.dma_start(CST[:, K_EARLY:K_ALL], consts[:, K_EARLY:K_ALL]).then_inc(late_in, 16)
            act.dma_start(LATE[:], late).then_inc(late_in, 16)
            act.wait_ge(pool_set, 1)
            nc.scalar.activation(WARM[:, 0:1], POWER[0:1, 0:1], ACT.Exp)
            n = 0
            for step in ACT_ORDER:
                b = step[1]
                ps = SMALL[b]
                if step[0] in ("spec", "back"):
                    h = step[2]
                    bank = AB[n % 2]
                    n += 1
                    act.wait_ge(a_full, n)
                    if step[0] == "spec":
                        dst, src = XF[:, b, HALF * h:HALF * (h + 1)], bank[0:C1, :]
                    else:
                        if b == 0 and h == 0:
                            act.wait_ge(pool_set, 7)
                        dst = PAD[:, b, 1 + ROWS * h:1 + ROWS * (h + 1), 1:1 + W]
                        src = bank[0:LANES, :].rearrange("c (y x) -> c y x", x=W)
                    nc.scalar.activation(dst, src, ACT.Copy).then_inc(a_free, 1)
                elif step[0] == "final":
                    h = step[2]
                    act.wait_ge(f_full, final_number(b, h) + 1)
                    act.wait_ge(bias_set, b + 1)
                    nc.scalar.activation(X[:, b, HALF * h:HALF * (h + 1)], FB[final_number(b, h) % 4][0:C, :],
                                         ACT.Identity, bias=col(b, BIAS)).then_inc(f_free, 1)
                elif step[0] == "shift":
                    act.wait_ge(shift_sum, b + 1)
                    nc.scalar.activation(WA[C:C1, b, :], ps[C:C1, 2 * C:4 * C], ACT.Copy).then_inc(wa_set, 1)
                    nc.scalar.activation(U[:, b, :], ps[0:C, P_U:P_U + 1], ACT.Copy).then_inc(u_set, 1)
                elif step[0] == "q1":
                    act.wait_ge(q1_sum, b + 1)
                    nc.scalar.activation(Q1[:, b, :], ps[0:C, 0:C], ACT.Copy).then_inc(q1_set, 1)
                elif step[0] == "square":
                    act.wait_ge(square_sum, b + 1)
                    nc.scalar.activation(S2[:, b, :], ps[0:C, P_SUMS + 2:P_SUMS + 4], ACT.Copy).then_inc(s2_set, 1)
                elif step[0] == "softmax":
                    act.wait_ge(logit_set, b + 1)
                    nc.scalar.activation(PR[:, b, :], LM[:, b, :], ACT.Exp, bias=col(b, NMAX),
                                         accum_out=col(b, SUM)).then_inc(exp_set, 1)
                elif step[0] == "tap":
                    act.wait_ge(a_free, through(A_STEPS, ("back", b, 1)))
                    if b == 0:
                        act.wait_ge(late_in, 16 * 2)
                    t, part = step[2:]
                    y, rows = tap_parts(b, part)
                    dy, dx = divmod(t, 3)
                    to = SCALED[:, slot(b, t), :] if t else ACC[:, b, :]
                    nc.scalar.activation(to[:, W * y:W * (y + rows)].rearrange("c (y x) -> c y x", x=W),
                                         PAD[:, b, y + dy:y + dy + rows, dx:dx + W], ACT.Copy,
                                         scale=LATE[0:LANES, L_DW + t:L_DW + t + 1]).then_inc(act_tap_set, 1)
                elif step[0] == "gelu":
                    h = step[2]
                    last = tap_step(b, h, TAPS - 1)
                    if TAPS - 1 in pool_taps(b):
                        act.wait_ge(pool_done, through(POOL_ORDER, last))
                    else:
                        act.wait_ge(tap_set, through(TAP_STEPS, last))
                    part = slice(HALF * h, HALF * (h + 1))
                    nc.scalar.activation(GE[:, b, part], ACC[GELU_AT:LANES, b, part], ACT.Gelu).then_inc(gelu_set, 1)

        @block.vector
        def _(dve):
            done = [0]

            def then(ins):
                done[0] += 1
                ins.then_inc(v_done, 1)
                dve.wait_ge(v_done, done[0])

            v = nc.vector
            for step in DVE_ORDER:
                name, b = step[0], step[1]
                ps = SMALL[b]
                if name == "gram":
                    dve.wait_ge(gram_sum, b + 1)
                    v.tensor_copy(G[:, b, 0:C1], ps[0:C1, P_GRAM:P_GRAM + C1]).then_inc(gram_set, 1)
                    dve.wait_ge(gram_set, b + 1)
                    if b == 0:
                        dve.wait_ge(early_in, 16)
                    else:
                        dve.wait_ge(diagonal_set, b)
                    v.scalar_tensor_tensor(DUMP[:], G[0:C, b, 0:C], 1.0, CST[0:C, K_IDENT:K_IDENT + C],
                                           ALU.mult, ALU.mult,
                                           accum_out=G[0:C, b, C1:C1 + 1]).then_inc(diagonal_set, 1)
                elif name == "var":
                    dve.wait_ge(group_mean, b + 1)
                    mean, square = ps[0:C, P_GROUP:P_GROUP + 1], ps[0:C, P_GROUP + 1:P_GROUP + 2]
                    then(v.tensor_scalar(col(b, NEGVAR), mean, mean, square, ALU.mult, ALU.subtract))
                    v.tensor_scalar(col(b, VAR), col(b, NEGVAR), -1.0, EPS, ALU.mult, ALU.add).then_inc(var_set, 1)
                    v.tensor_scalar(col(b, NEGMEAN), mean, -1.0, None, ALU.mult).then_inc(negmean_set, 1)
                elif name == "norm":
                    dve.wait_ge(negmean_set, b + 1)
                    dve.wait_ge(pool_done, through(POOL_ORDER, ("var", b)))
                    v.tensor_tensor(col(b, SHIFT), col(b, NEGMEAN), col(b, RSTD), ALU.mult).then_inc(shift_set, 1)
                    if b == 0:
                        dve.wait_ge(weights_in, 16)
                    v.tensor_scalar(WA[0:C, b, :], WTS[0:C, W_QK:W_QK + 2 * C], col(b, RSTD), None,
                                    ALU.mult).then_inc(scaled_set, 1)
                elif name == "setup":
                    dve.wait_ge(filter_sum, 1)
                    v.tensor_copy(FREAL[:], VB[0][:, 0:C]).then_inc(filter_set, 1)
                    dve.wait_ge(late_in, 16 * 2)
                    for t in range(max(PE_TAPS)):
                        v.tensor_scalar(DIAG[:, t, :], CST[0:LANES, K_IDENT:K_IDENT + LANES], LATE[0:LANES, L_DW + t:L_DW + t + 1],
                                        None, ALU.mult).then_inc(diag_set, 1)
                elif name == "project":
                    dve.wait_ge(qk_sum, b + 1)
                    dve.wait_ge(scaled_set, b + 1)
                    dve.wait_ge(wa_set, b + 1)
                    v.tensor_copy(TK[:, b, :], ps[0:C1, C:2 * C]).then_inc(qk_set, 1)
                    v.tensor_tensor(QQ[:, b, :], WA[:, b, :], ps[0:C1, 0:2 * C], ALU.mult).then_inc(qk_set, 1)
                elif name == "logits":
                    dve.wait_ge(logit_sum, b + 1)
                    v.tensor_scalar(NRM[:, b, :], ps[0:C, P_SUMS:P_SUMS + 2], L2_EPS * L2_EPS, None,
                                    ALU.max).then_inc(norm_set, 1)
                elif name == "scale":
                    dve.wait_ge(pool_done, through(POOL_ORDER, ("logits", b)))
                    v.tensor_scalar(KL[:, b, :], ps[0:C, 2 * C:3 * C], RN[:, b, 1:2], None,
                                    ALU.mult).then_inc(kl_set, 1)
                    v.tensor_tensor(col(b, RQ), RN[:, b, 0:1], WTS[0:C, W_TEMP:W_TEMP + 1], ALU.mult).then_inc(rq_set, 1)
                elif name == "softmax":
                    dve.wait_ge(turned_sum, b + 1)
                    dve.wait_ge(rq_set, b + 1)
                    if b == 0:
                        dve.wait_ge(late_in, 16 * 2)
                    then(v.scalar_tensor_tensor(LM[:, b, :], ps[0:C, 3 * C:4 * C], col(b, RQ),
                                                CST[0:C, K_MASK:K_MASK + C], ALU.mult, ALU.add))
                    v.tensor_reduce(col(b, NMAX), LM[:, b, :], AX.X, ALU.max, negate=True).then_inc(logit_set, 1)
                elif name == "attend":
                    dve.wait_ge(exp_set, b + 1)
                    then(v.reciprocal(col(b, RSUM), col(b, SUM)))
                    v.tensor_scalar(PJ[:, b, :], WTS[0:C, W_PROJ:W_PROJ + C], col(b, RSUM), None, ALU.mult).then_inc(attn_set, 1)
                elif name == "mix":
                    dve.wait_ge(m_sum, b + 1)
                    if b == 0:
                        dve.wait_ge(pool_set, 3)
                    v.scalar_tensor_tensor(AT[:, b, :], ps[0:C1, 2 * C:3 * C], ST[:, b, RSTD:RSTD + 1],
                                           WTS[:, W_IDENT:W_IDENT + C], ALU.mult, ALU.add).then_inc(at_set, 1)
                    v.tensor_copy(M[:, b, 0:C], ps[0:C, 3 * C:4 * C]).then_inc(m_set, 1)
                    v.tensor_tensor(col(b, BIAS), ps[0:C, P_SUMS:P_SUMS + 1], WTS[0:C, W_BIAS:W_BIAS + 1],
                                    ALU.add).then_inc(bias_set, 1)
                elif name == "second":
                    dve.wait_ge(ag_sum, b + 1)
                    dve.wait_ge(at_set, b + 1)
                    v.tensor_tensor(AGA[:, b, :], AT[:, b, :], ps[0:C1, 0:C], ALU.mult).then_inc(aga_set, 1)
                elif name == "group":
                    dve.wait_ge(group2_sum, b + 1)
                    mean, square = ps[0:C, P_GROUP:P_GROUP + 1], ps[0:C, P_GROUP + 1:P_GROUP + 2]
                    then(v.tensor_scalar(V2[:, b, :], mean, mean, square, ALU.mult, ALU.subtract))
                    v.tensor_scalar(col(b, V2E), V2[:, b, :], -1.0, EPS, ALU.mult, ALU.add).then_inc(var2_set, 1)
                    dve.wait_ge(bias_set, b + 1)
                    v.tensor_scalar(M[:, b, C:C1], mean, -1.0, col(b, BIAS), ALU.mult, ALU.add).then_inc(column_set, 1)
                elif name == "weigh":
                    dve.wait_ge(pool_done, through(POOL_ORDER, ("group", b)))
                    v.tensor_scalar(WI[0:C, b, :], WTS[0:C, W_IN:W_IN + C], col(b, R2), None,
                                    ALU.mult).then_inc(wi_set, 1)
                elif name == "fold":
                    dve.wait_ge(bt_sum, b + 1)
                    dve.wait_ge(wi_set, b + 1)
                    if b == 0:
                        dve.wait_ge(pool_set, 4)
                    v.scalar_tensor_tensor(BT[:, b, :], ps[0:C1, C:2 * C], ST[:, b, RSTD:RSTD + 1],
                                           WI[:, b, :], ALU.mult, ALU.add).then_inc(bt_set, 1)
                elif name == "filter":
                    h, n = step[2], through(V_STEPS, step)
                    dve.wait_ge(v_full, n)
                    if b == 0 and h == 0:
                        dve.wait_ge(filter_set, 1)
                    zs = Z[:, b, STRIPS * h:STRIPS * (h + 1), :]
                    for first, at in ((0, 0), (GATED, GELU_AT)):
                        ins = v.tensor_tensor(
                            zs[:, :, at:at + GATED],
                            VB[(n - 1) % 2][:, 0:STRIPS * C].rearrange("p (s c) -> p s c", c=C)[
                                :, :, first:first + GATED],
                            FREAL[:, first:first + GATED].unsqueeze(1).broadcast_to([2 * FREQ, STRIPS, GATED]),
                            ALU.mult)
                    ins.then_inc(v_free, 1)
                elif name == "tap":
                    t, part = step[2:]
                    y, rows = tap_parts(b, part)
                    acc = ACC[:, b, W * y:W * (y + rows)].rearrange("c (y x) -> c y x", x=W)
                    before = acc
                    if t - 1 in pool_taps(b):
                        dve.wait_ge(pool_done, through(POOL_ORDER, ("tap", b, t - 1, part)))
                    elif t > max(PE_TAPS[b], 1):
                        dve.wait_ge(tap_set, through(TAP_STEPS, ("tap", b, t - 1, part)))
                    elif PE_TAPS[b]:
                        dve.wait_ge(conv_sum, through(CONV_STEPS, ("conv", b, part if PARTS[b] == 2 else 1)))
                        before = (CV[0:LANES, part, :] if PARTS[b] == 2 else
                                  CV[0:LANES, :, :].rearrange("c h n -> c (h n)")).rearrange(
                                      "c (y x) -> c y x", x=W)
                    else:
                        dve.wait_ge(act_tap_set, through(ACT_TAP_STEPS, ("tap", b, 0, part)))
                    dy, dx = divmod(t, 3)
                    v.scalar_tensor_tensor(acc, PAD[:, b, y + dy:y + dy + rows, dx:dx + W], LATE[0:LANES, L_DW + t:L_DW + t + 1],
                                           before, ALU.mult, ALU.add).then_inc(tap_set, 1)
                elif name == "gate":
                    h = step[2]
                    dve.wait_ge(gelu_set, through(GELU_STEPS, ("gelu", b, h)))
                    part = slice(HALF * h, HALF * (h + 1))
                    v.tensor_tensor(GT[:, b, part], GE[:, b, part], ACC[0:GATED, b, part],
                                    ALU.mult).then_inc(gate_set, 1)

        @block.tensor
        def _(pe):
            def mm(o, lhsT, rhs, start=True, stop=True):
                return nc.tensor.matmul(o, lhsT, rhs, start=start, stop=stop)

            ident = CST[0:C, K_IDENT:K_IDENT + C]
            group = CST[0:C, K_GROUP:K_GROUP + C]
            for step in PE_ORDER:
                name, b = step[0], step[1]
                ps = SMALL[b]
                if name in ("spec", "back"):
                    h, n = step[2], through(A_STEPS, step)
                    bank = AB[(n - 1) % 2]
                    if n > 2:
                        pe.wait_ge(a_free, n - 2)
                    if name == "spec":
                        pe.wait_ge(xt_in[b], 16)
                        if b == 0 and h == 0:
                            pe.wait_ge(first_in, 16)
                            pe.wait_ge(early_in, 16)
                        for s in range(STRIPS):
                            ins = mm(bank[0:C1, STRIP * s:STRIP * (s + 1)], XT[:, b, STRIPS * h + s, :],
                                     CST[:, K_DFT:K_DFT + 2 * FREQ])
                    else:
                        pe.wait_ge(v_free, through(V_STEPS, ("filter", b, h)))
                        if b == 0 and h == 0:
                            pe.wait_ge(pool_set, 5)
                        rows = bank[0:LANES, :].rearrange("c (y s x) -> c s y x", s=STRIPS, x=P)
                        for s in range(STRIPS):
                            ins = mm(rows[:, s], Z[:, b, STRIPS * h + s, :], CST[:, K_BACK:K_BACK + 2 * FREQ])
                    ins.then_inc(a_full, 1)
                elif name == "base":
                    h = step[2]
                    n = final_number(b, h)
                    pe.wait_ge(x_in[b], 16)
                    pe.wait_ge(at_set, b + 1)
                    if n < 2:
                        pe.wait_ge(bt_set, n + 1)
                    elif n < 4:
                        pe.wait_ge(v_free, len(V_STEPS))
                    else:
                        pe.wait_ge(f_free, n - 3)
                    mm(FB[n % 4][0:C, :], AT[0:C, b, :], X[:, b, HALF * h:HALF * (h + 1)], stop=False)
                elif name == "final":
                    h = step[2]
                    if b < POOL_GATES:
                        pe.wait_ge(pool_done, through(POOL_ORDER, ("gate", b, h)))
                    else:
                        pe.wait_ge(gate_set, through(GATE_STEPS, ("gate", b, h)))
                    mm(FB[final_number(b, h) % 4][0:C, :], LATE[0:GATED, L_OUT:L_OUT + C],
                       GT[:, b, :].rearrange("p (h y s x) -> p h s y x", h=2, y=ROWS, x=P)[:, h],
                       start=False).then_inc(f_full, 1)
                elif name == "gram":
                    if b == 0:
                        pe.wait_ge(first_in, 16)
                    for s in range(2 * STRIPS):
                        if s == (STRIPS if b == 0 else 0):
                            pe.wait_ge(xt_in[b], 16)
                        ins = mm(ps[0:C1, P_GRAM:P_GRAM + C1], XT[:, b, s, :], XT[:, b, s, :], start=(s == 0),
                                 stop=(s == 2 * STRIPS - 1))
                    ins.then_inc(gram_sum, 1)
                elif name == "stats":
                    pe.wait_ge(gram_set, b + 1)
                    pe.wait_ge(diagonal_set, b + 1)
                    if b == 0:
                        pe.wait_ge(early_in, 16)
                    mm(ps[0:C, P_GROUP:P_GROUP + 2], group, G[0:C, b, C:C1 + 1]).then_inc(group_mean, 1)
                elif name == "shift":
                    pe.wait_ge(shift_set, b + 1)
                    pe.wait_ge(negmean_set, b + 1)
                    if b == 0:
                        pe.wait_ge(weights_in, 16)
                    mm(ps[C:C1, 2 * C:4 * C], col(b, SHIFT), WTS[0:C, W_QK:W_QK + 2 * C])
                    mm(ps[0:C, P_U:P_U + 1], WTS[0:C, W_VT:W_VT + C], col(b, SHIFT)).then_inc(shift_sum, 1)
                elif name == "setup":
                    pe.wait_ge(late_in, 16 * 2)
                    mm(VB[0][:, 0:C], CST[0:P * (P // 2 + 1), K_SEL:K_SEL + 2 * FREQ], LATE[0:P * (P // 2 + 1), L_FILTER:L_FILTER + C]).then_inc(filter_sum, 1)
                elif name == "project":
                    pe.wait_ge(scaled_set, b + 1)
                    pe.wait_ge(wa_set, b + 1)
                    pe.wait_ge(u_set, b + 1)
                    mm(ps[0:C1, 0:2 * C], G[:, b, 0:C1], WA[:, b, :]).then_inc(qk_sum, 1)
                elif name == "logits":
                    pe.wait_ge(qk_set, 2 * (b + 1))
                    if b == 0:
                        pe.wait_ge(pool_set, 2)
                    mm(ps[0:C, P_SUMS:P_SUMS + 1], QQ[:, b, 0:C], ONES[:])
                    mm(ps[0:C, P_SUMS + 1:P_SUMS + 2], QQ[:, b, C:2 * C], ONES[:])
                    mm(ps[0:C, 2 * C:3 * C], TK[:, b, :], WA[:, b, 0:C]).then_inc(logit_sum, 1)
                elif name == "softmax":
                    pe.wait_ge(kl_set, b + 1)
                    mm(ps[0:C, 3 * C:4 * C], KL[:, b, :], ident).then_inc(turned_sum, 1)
                elif name == "attend":
                    pe.wait_ge(attn_set, b + 1)
                    mm(ps[0:C, 0:C], PR[:, b, :], PJ[:, b, :]).then_inc(q1_sum, 1)
                elif name == "mix":
                    pe.wait_ge(q1_set, b + 1)
                    mm(ps[0:C, 2 * C:3 * C], WTS[0:C, W_V:W_V + C], Q1[:, b, :])
                    mm(ps[C:C1, 2 * C:3 * C], U[:, b, :], Q1[:, b, :])
                    mm(ps[0:C, 3 * C:4 * C], Q1[:, b, :], WTS[0:C, W_V:W_V + C])
                    mm(ps[0:C, P_SUMS:P_SUMS + 1], Q1[:, b, :], U[:, b, :]).then_inc(m_sum, 1)
                elif name == "second":
                    pe.wait_ge(at_set, b + 1)
                    pe.wait_ge(bias_set, b + 1)
                    mm(ps[0:C, P_SUMS + 2:P_SUMS + 3], AT[:, b, :], G[:, b, C:C1])
                    mm(ps[0:C1, 0:C], G[:, b, 0:C1], AT[:, b, :]).then_inc(ag_sum, 1)
                elif name == "square":
                    pe.wait_ge(aga_set, b + 1)
                    mm(ps[0:C, P_SUMS + 3:P_SUMS + 4], AGA[:, b, :], ONES[:]).then_inc(square_sum, 1)
                elif name == "group":
                    pe.wait_ge(s2_set, b + 1)
                    mm(ps[0:C, P_GROUP:P_GROUP + 2], group, S2[:, b, :]).then_inc(group2_sum, 1)
                elif name == "fold":
                    pe.wait_ge(m_set, b + 1)
                    pe.wait_ge(column_set, b + 1)
                    pe.wait_ge(wi_set, b + 1)
                    mm(ps[0:C1, C:2 * C], M[:, b, :], WI[0:C, b, :]).then_inc(bt_sum, 1)
                elif name == "filter":
                    h, n = step[2], through(V_STEPS, step)
                    pe.wait_ge(bt_set, b + 1)
                    pe.wait_ge(a_free, through(A_STEPS, ("spec", b, h)))
                    pe.wait_ge(filter_set, 1)
                    if n > 2:
                        pe.wait_ge(v_free, n - 2)
                    for s in range(STRIPS):
                        at = HALF * h + STRIP * s
                        ins = mm(VB[(n - 1) % 2][:, C * s:C * (s + 1)], XF[:, b, at:at + STRIP], BT[:, b, :])
                    ins.then_inc(v_full, 1)
                elif name == "conv":
                    h = step[2]
                    pe.wait_ge(a_free, through(A_STEPS, ("back", b, 1)))
                    earlier = [i for i in range(b) if PE_TAPS[i]]
                    if not earlier:
                        pe.wait_ge(bt_set, B)
                        pe.wait_ge(diag_set, max(PE_TAPS))
                    else:
                        i = earlier[-1]
                        pe.wait_ge(tap_set, through(TAP_STEPS, tap_step(i, h, PE_TAPS[i])))
                    for t in range(PE_TAPS[b]):
                        dy, dx = divmod(t, 3)
                        ins = mm(CV[0:LANES, h, :], DIAG[:, t, :],
                                 PAD[:, b, ROWS * h + dy:ROWS * (h + 1) + dy, dx:dx + W],
                                 start=(t == 0), stop=(t == PE_TAPS[b] - 1))
                    ins.then_inc(conv_sum, 1)



def kernel(**inputs):
    import concourse.bacc as bacc
    from concourse.bass_utils import run_bass_kernel_spmd

    f32 = np.float32
    qkv = np.asarray(inputs["L0_conv_qkv_w"])
    gates_first = np.r_[GATED:C, 0:GATED]
    x = np.asarray(inputs["x"]).reshape(B, C, 2, ROWS, STRIPS, P).transpose(0, 1, 2, 4, 3, 5)
    weights = np.zeros((C1, W_ALL), f32)
    weights[:C, W_QK:W_QK + 2 * C] = qkv[:2 * C].T
    weights[:C, W_V:W_V + C] = qkv[2 * C:]
    weights[:C, W_VT:W_VT + C] = qkv[2 * C:].T
    weights[:C, W_PROJ:W_PROJ + C] = np.asarray(inputs["L0_conv_proj_w"]).T
    weights[:C, W_IN:W_IN + C] = np.asarray(inputs["L1_conv_w_in"]).T[:, gates_first]
    weights[:C, W_IDENT:W_IDENT + C] = np.eye(C)
    weights[C, W_IDENT:W_IDENT + C] = np.asarray(inputs["L0_conv_proj_b"])
    weights[:C, W_BIAS] = np.asarray(inputs["L0_conv_proj_b"])
    weights[:C, W_TEMP] = np.repeat(np.asarray(inputs["L0_conv_temperature"]).reshape(HEADS), HD)
    late = np.zeros((128, L_ALL), f32)
    late[:P * (P // 2 + 1), L_FILTER:L_FILTER + C] = (
        np.asarray(inputs["L1_conv_fft_filter"]).reshape(C, P * (P // 2 + 1)).T[:, gates_first])
    late[:GATED, L_OUT:L_OUT + C] = np.asarray(inputs["L1_conv_w_out"]).T
    taps = np.asarray(inputs["L1_conv_w_dw"]).reshape(C, TAPS)
    late[:GATED, L_DW:L_DW + TAPS] = taps[GATED:]
    late[GELU_AT:LANES, L_DW:L_DW + TAPS] = taps[:GATED]
    xT = np.ones((B, STRIP, 2 * STRIPS, C1), f32)
    xT[..., :C] = x.reshape(B, C, 2 * STRIPS, STRIP).transpose(0, 3, 2, 1)
    arrays = {
        "x": x.reshape(B, C, PIX),
        "xT": xT,
        "consts": constants(),
        "weights": weights,
        "late": late,
    }
    arrays = {f"in_{k}": np.ascontiguousarray(v) for k, v in arrays.items()}
    nc = bacc.Bacc("TRN2", target_bir_lowering=False, num_devices=1)
    args = [nc.dram_tensor(k, v.shape, mybir.dt.from_np(v.dtype), kind="ExternalInput").ap()
            for k, v in arrays.items()]
    out = nc.dram_tensor("out", [B, C, PIX], F32, kind="ExternalOutput").ap()
    build(nc, *args, out)
    r = run_bass_kernel_spmd(nc, [arrays], core_ids=[0])
    got = np.asarray(r.results[0]["out"])
    return got.reshape(B, C, 2, STRIPS, ROWS, P).transpose(0, 1, 2, 4, 3, 5).reshape(B, C, H, W)
```
